# Optimizing a Trainium2 kernel written in Bass

```python
import numpy as np
import jax
import jax.numpy as jnp

def _softmax(x, axis=-1):
    return jax.nn.softmax(x, axis=axis)

def _gelu(x):
    return jax.nn.gelu(x, approximate=True)

def _silu(x):
    return jax.nn.silu(x)

def _sigmoid(x):
    return jax.nn.sigmoid(x)

def _layernorm(x, axis=-1, eps=1e-05):
    m = jnp.mean(x, axis=axis, keepdims=True)
    v = jnp.var(x, axis=axis, keepdims=True)
    return (x - m) / jnp.sqrt(v + eps)

def _scatter_add(tgt, idx, src, axis=0):
    return tgt.at[idx].add(src)

def _segment_sum(src, seg, n):
    return jax.ops.segment_sum(src, seg, n)
kernel_name = 'mk_macaron_d1_jaxref_r8_b0f5b7'

def setup_inputs(seed: int=0):
    np.random.seed(seed)
    _w = jnp.asarray

    def _L0_attn_setup():
        import jax, jax.numpy as jnp
        import numpy as np
        import math
        B, T, C, H = (2, 256, 128, 16)
        key = jax.random.key(seed)
        ks = jax.random.split(key, 5)
        s = 0.02
        return {'x': jax.random.normal(ks[0], (B, T, C), dtype=jnp.float32), 'W_attn': jax.random.normal(ks[1], (C, 3 * C), dtype=jnp.float32) * s, 'b_attn': jnp.zeros((3 * C,), dtype=jnp.float32), 'W_proj': jax.random.normal(ks[2], (C, C), dtype=jnp.float32) * s, 'b_proj': jnp.zeros((C,), dtype=jnp.float32)}
    _L0_attn_in = _L0_attn_setup()

    def _L0_ffn_setup():
        import jax, jax.numpy as jnp
        import numpy as np
        B, S, H = (1, 128, 128)
        E = 128
        NEXP = 16
        TOPK = 2
        ALPHA = 1.702
        LIMIT = 7.0

        def _moe_forward(x, Wg, bg, Wgu, bgu, Wd, bd):
            b, s, h = x.shape
            xt = x.reshape(-1, h)
            logits = xt @ Wg.T + bg
            top_vals, top_idx = jax.lax.top_k(logits, TOPK)
            rw = jax.nn.softmax(top_vals.astype(jnp.float32), axis=-1).astype(xt.dtype)
            onehot = jax.nn.one_hot(top_idx, NEXP, dtype=xt.dtype)
            cw = jnp.einsum('tk,tke->te', rw, onehot)
            gu = jnp.einsum('th,ehf->tef', xt, Wgu) + bgu[None]
            gate = gu[..., ::2]
            up = gu[..., 1::2]
            gate = jnp.minimum(gate, LIMIT)
            up = jnp.clip(up, -LIMIT, LIMIT)
            glu = gate * jax.nn.sigmoid(gate * ALPHA)
            gated = (up + 1.0) * glu
            out_e = jnp.einsum('tef,efh->teh', gated, Wd) + bd[None]
            out = jnp.einsum('teh,te->th', out_e, cw)
            return out.reshape(b, s, h)
        key = jax.random.key(seed)
        ks = jax.random.split(key, 8)
        hidden_states = jax.random.normal(ks[0], (B, S, H), dtype=jnp.float32)
        Wg = jax.random.normal(ks[1], (NEXP, H), dtype=jnp.float32) / np.sqrt(H)
        bg = jax.random.normal(ks[2], (NEXP,), dtype=jnp.float32) * 0.01
        Wgu = jax.random.normal(ks[3], (NEXP, H, 2 * E), dtype=jnp.float32) / np.sqrt(H)
        bgu = jax.random.normal(ks[4], (NEXP, 2 * E), dtype=jnp.float32) * 0.01
        Wd = jax.random.normal(ks[5], (NEXP, E, H), dtype=jnp.float32) / np.sqrt(E)
        bd = jax.random.normal(ks[6], (NEXP, H), dtype=jnp.float32) * 0.01
        return {'hidden_states': hidden_states, 'Wg': Wg, 'bg': bg, 'Wgu': Wgu, 'bgu': bgu, 'Wd': Wd, 'bd': bd}
    _L0_ffn_in = _L0_ffn_setup()
    _d = {'L0_attn_x': _L0_attn_in['x'], 'L0_attn_W_attn': _L0_attn_in['W_attn'], 'L0_attn_b_attn': _L0_attn_in['b_attn'], 'L0_attn_W_proj': _L0_attn_in['W_proj'], 'L0_attn_b_proj': _L0_attn_in['b_proj'], 'L0_ffn_Wg': _L0_ffn_in['Wg'], 'L0_ffn_bg': _L0_ffn_in['bg'], 'L0_ffn_Wgu': _L0_ffn_in['Wgu'], 'L0_ffn_bgu': _L0_ffn_in['bgu'], 'L0_ffn_Wd': _L0_ffn_in['Wd'], 'L0_ffn_bd': _L0_ffn_in['bd']}
    _x0 = _d['L0_attn_x']
    _d['L0_attn_x'] = jax.random.normal(jax.random.fold_in(jax.random.key(seed), 1), (16, 256, 128), dtype=_x0.dtype)
    del _x0
    return _d

def reference(L0_attn_x, L0_attn_W_attn, L0_attn_b_attn, L0_attn_W_proj, L0_attn_b_proj, L0_ffn_Wg, L0_ffn_bg, L0_ffn_Wgu, L0_ffn_bgu, L0_ffn_Wd, L0_ffn_bd):

    def _L0_attn_ref(x, W_attn, b_attn, W_proj, b_proj):
        import jax, jax.numpy as jnp
        import numpy as np
        import math
        B, T, C, H = (2, 256, 128, 16)
        Bx, Tx, Cx = x.shape
        hd = Cx // H
        qkv = x @ W_attn + b_attn
        q, k, v = jnp.split(qkv, 3, axis=-1)
        q = q.reshape(Bx, Tx, H, hd).transpose(0, 2, 1, 3)
        k = k.reshape(Bx, Tx, H, hd).transpose(0, 2, 1, 3)
        v = v.reshape(Bx, Tx, H, hd).transpose(0, 2, 1, 3)
        scale = 1.0 / math.sqrt(hd)
        att = jnp.einsum('bhqd,bhkd->bhqk', q, k) * scale
        causal = jnp.tril(jnp.ones((Tx, Tx), dtype=bool))
        att = jnp.where(causal[None, None, :, :], att, -jnp.inf)
        att = jax.nn.softmax(att, axis=-1)
        y = jnp.einsum('bhqk,bhkd->bhqd', att, v)
        y = y.transpose(0, 2, 1, 3).reshape(Bx, Tx, Cx)
        return y @ W_proj + b_proj

    def _L0_ffn_ref(hidden_states, Wg, bg, Wgu, bgu, Wd, bd):
        import jax, jax.numpy as jnp
        import numpy as np
        B, S, H = (1, 128, 128)
        E = 128
        NEXP = 16
        TOPK = 2
        ALPHA = 1.702
        LIMIT = 7.0

        def _moe_forward(x, Wg, bg, Wgu, bgu, Wd, bd):
            b, s, h = x.shape
            xt = x.reshape(-1, h)
            logits = xt @ Wg.T + bg
            top_vals, top_idx = jax.lax.top_k(logits, TOPK)
            rw = jax.nn.softmax(top_vals.astype(jnp.float32), axis=-1).astype(xt.dtype)
            onehot = jax.nn.one_hot(top_idx, NEXP, dtype=xt.dtype)
            cw = jnp.einsum('tk,tke->te', rw, onehot)
            gu = jnp.einsum('th,ehf->tef', xt, Wgu) + bgu[None]
            gate = gu[..., ::2]
            up = gu[..., 1::2]
            gate = jnp.minimum(gate, LIMIT)
            up = jnp.clip(up, -LIMIT, LIMIT)
            glu = gate * jax.nn.sigmoid(gate * ALPHA)
            gated = (up + 1.0) * glu
            out_e = jnp.einsum('tef,efh->teh', gated, Wd) + bd[None]
            out = jnp.einsum('teh,te->th', out_e, cw)
            return out.reshape(b, s, h)
        return _moe_forward(hidden_states, Wg, bg, Wgu, bgu, Wd, bd)
    x = L0_attn_x
    x = x + 0.5 * _L0_ffn_ref(_layernorm(x, axis=-1), L0_ffn_Wg, L0_ffn_bg, L0_ffn_Wgu, L0_ffn_bgu, L0_ffn_Wd, L0_ffn_bd)
    x = x + _L0_attn_ref(_layernorm(x, axis=-1), L0_attn_W_attn, L0_attn_b_attn, L0_attn_W_proj, L0_attn_b_proj)
    x = x + 0.5 * _L0_ffn_ref(_layernorm(x, axis=-1), L0_ffn_Wg, L0_ffn_bg, L0_ffn_Wgu, L0_ffn_bgu, L0_ffn_Wd, L0_ffn_bd)
    return x

_drawn_inputs = setup_inputs


def setup_inputs(seed=0):
    import zlib

    import numpy as np

    out = dict(_drawn_inputs(seed))
    spreads = {'L0_attn_b_attn': (0.0, 0.1), 'L0_attn_b_proj': (0.0, 0.1)}
    factors = {'L0_attn_W_attn': 3.327, 'L0_ffn_bgu': 3.824, 'L0_ffn_bd': 4.164}
    for name, (base, spread) in spreads.items():
        noise = np.random.default_rng([zlib.crc32(name.encode()), seed]).standard_normal(out[name].shape)
        drawn = base * np.exp(spread * noise) if base else spread * noise
        out[name] = jnp.asarray(drawn.astype(out[name].dtype))
    for name, factor in factors.items():
        out[name] = (out[name] * factor).astype(out[name].dtype)
    return out
```

```python
from contextlib import ExitStack

import numpy as np

import concourse.bass as bass
from concourse import mybir

F32 = mybir.dt.float32
F32R = mybir.dt.float32r
BF16 = mybir.dt.bfloat16
I32 = mybir.dt.int32
U32 = mybir.dt.uint32
ALU = mybir.AluOpType
ACT = mybir.ActivationFunctionType
AX = mybir.AxisListType

P = 128
B, T, C = 16, 256, 128
N = B * T
NT = N // P
QUAD = 4
NQ = NT // QUAD
E, TOPK, F = 16, 2, 128
REGION = N + P
TILES = N * TOPK // P + E
UNROLL = 4
TURNS = TILES // UNROLL
ALPHA, LIMIT, EPS = 1.702, 7.0, 1e-5
ROUND = 1.5 * 2.0 ** 23
EW = 2 * F + C
NEG = -1e30
H, D = 16, 8
SCALE = D ** -0.5
GRP = 4
QT = T // P
V1 = D + 1
SLOTS = 4
UNITS = SLOTS * GRP
TURNS_A = B // SLOTS
STACKED = 2 * 4 * 4 * 16

K_ID, K_TRI = 0, 128
K_E, K_BASE, K_ROW, K_ROW128, K_BASEP = 256, 272, 288, 289, 290
K_U = 291
K_MQ, K_MK = 323, 451
K_SEL = 579
K_W = K_SEL + 8 * P


def shape_constants():
    p = np.arange(P)
    k = np.zeros((P, K_W), np.float32)
    k[:, K_ID:K_ID + P] = np.eye(P)
    k[:, K_TRI:K_TRI + P] = p[:, None] < p[None, :]
    k[:, K_E:K_E + E] = np.arange(E)
    k[:, K_BASE:K_BASE + E] = np.arange(E) * REGION
    k[:, K_ROW] = p
    k[:, K_ROW128] = p * P
    k[:, K_BASEP] = p * REGION
    e = np.arange(E)
    k[:E, K_U:K_U + E] = e[:, None] <= e[None, :]
    k[:E, K_U + E:K_U + 2 * E] = e[:, None] < e[None, :]
    k[:, K_MQ:K_MQ + P] = np.where(p[None, :] > p[:, None], NEG, 0)
    k[:, K_MK:K_MK + P] = np.where(p[:, None] > p[None, :], NEG, 0)
    for qt in range(2):
        for g in range(4):
            for part in range(2):
                c = K_SEL + (qt * 4 + g) * P
                k[qt * 8 + part * 4 + g, c:c + P] = 1
    return k


class Chain:

    def __init__(self, eng, sem):
        self.eng, self.sem, self.count, self.turns = eng, sem, 0, 0

    def mark(self, ins):
        ins.then_inc(self.sem, 1)
        self.count += 1
        return self.count + self.turns

    def wait(self, value=None):
        self.eng.wait_ge(self.sem, self.count + self.turns if value is None else value)

    def begin(self, turn, per_turn):
        self.start, self.per_turn = self.count, per_turn
        self.turns = turn * per_turn

    def end(self, turns):
        assert self.count - self.start == self.per_turn, (self.count - self.start, self.per_turn)
        self.count = self.start + turns * self.per_turn
        self.turns = 0


def build_block(nc, x, w_g, b_g, w_gu, w_d, b_gu, b_d, b_attn, b_proj, w_attn, w_proj, konst, out):
    ctx = ExitStack()
    with ctx:
        def sb(name, shape, dt=F32):
            return ctx.enter_context(nc.sbuf_tensor(name, shape, dt))

        def sem(name):
            return ctx.enter_context(nc.semaphore(name))

        banks = ctx.enter_context(nc.psum_tensor("banks", [P, 8, 512], F32))
        bank = [banks[:, i, :] for i in range(8)]

        rows_dram = nc.dram_tensor("rows_by_expert", (E * REGION, C), F32, kind="Internal").ap()
        results_dram = nc.dram_tensor("results_by_tile", (TILES * P, C), F32, kind="Internal").ap()

        xs = sb("x_resident", [P, QT + NT, C])
        xr = xs[:, QT:, :]
        kc = sb("konst_sb", [P, K_W])
        ident = kc[:, K_ID:K_ID + P]
        tri = sb("tri", [P, P], BF16)
        ones = sb("ones", [P, P], BF16)
        utri = sb("utri", [E, 2 * E], BF16)
        wg = sb("wg", [P, E])
        bg = sb("bg", [P, E])
        wgu = sb("wgu", [P, E * 2 * F])
        wd = sb("wd", [P, E * C])
        zeros = sb("zeros", [P, C])
        NB = E + 1
        bias_in = sb("bias_in", [NB, EW])
        bias_hi = sb("bias_hi", [NB, EW], BF16)
        bias_mid = sb("bias_mid", [NB, EW], BF16)
        bias_lo = sb("bias_lo", [NB, EW], BF16)
        bias_r1 = sb("bias_r1", [NB, EW])
        bias_r2 = sb("bias_r2", [NB, EW])
        bias3 = sb("bias3", [3, NB * EW], BF16)

        xn = sb("xn", [P, NT, C])
        st6 = sb("st6", [P, NT, 6])
        mv = sb("mv", [P, NT, 2])
        veps = sb("veps", [P, NT])
        rstd = sb("rstd", [P, NT])
        neghalf = sb("neghalf", [P, QUAD])
        xnT = sb("xnT", [P, 2, QUAD * P])
        lg = sb("lg", [P, NQ, QUAD, E])
        mx = sb("mx", [P, NT, 8])
        mi = sb("mi", [P, NT, 8], U32)
        mif = sb("mif", [P, NT, TOPK])
        oh = sb("oh", [P, NT, TOPK, E], BF16)
        mask = sb("mask", [P, NT, E], BF16)
        macc = sb("macc", [P, NQ + 1, E], BF16)
        msum = sb("msum", [P, NQ, E])
        gap = sb("gap", [P, NT])
        rank = sb("rank", [P, NQ, QUAD, E])
        rsel = sb("rsel", [P, NQ, QUAD * TOPK, E])
        posf = sb("posf", [P, NT * TOPK])
        posi = sb("posi", [P, NT * TOPK], I32)
        wts = sb("wts", [P, TOPK, NT])
        cnt = sb("cnt", [E, P])
        cntr = sb("cntr", [E, P])
        ntile = sb("ntile", [E, P], BF16)
        cum = sb("cum", [P, 2 * E])
        delta = sb("delta", [P, E])
        below = sb("below", [P, 2 * E])
        hot = sb("hot", [P, E])
        rowof = sb("rowof", [P, E])
        tmp2 = sb("tmp2", [P, 2, E])
        tabf = sb("tabf", [P, 2])
        tabc = sb("tabc", [P, 2], I32)
        zrow = sb("zrow", [E, 1], I32)
        tab = sb("tab", [1, 2 * TILES + E], I32)
        dsel = sb("dsel", [P, NT * TOPK, E])
        dsum = sb("dsum", [P, NT * TOPK])
        resi = sb("resi", [P, NT * TOPK], I32)
        xt = sb("xt", [P, UNROLL, C])
        xT = sb("xT", [P, 2, 2 * P])
        sig = sb("sig", [P, 2, 2, F])
        glu = sb("glu", [P, 2, 2, F])
        upc = sb("upc", [P, 2, 2, F])
        gated = sb("gated", [P, 2, 2, F])
        gT = sb("gT", [P, 2, 2 * P])
        ysb = sb("ysb", [P, 2, 2, C])
        w_in = sb("w_attn_sb", [P, 3 * C])
        w_out = sb("w_proj_sb", [P, C])
        bqk = sb("bqk", [P, 2])
        identb = sb("identb", [P, P], BF16)
        mask_q = sb("mask_q", [P, P], BF16)
        mask_k = sb("mask_k", [P, P], BF16)
        select = sb("select", [P, QT * GRP, P], F32R)
        a_st6 = sb("a_st6", [P, QUAD, 6])
        a_mv = sb("a_mv", [P, QUAD, 2])
        a_ve = sb("a_ve", [P, QUAD])
        a_rs = sb("a_rs", [P, QUAD])
        xa = sb("xa", [P, QUAD, C])
        xaT = sb("xaT", [P, QUAD * P])
        hl = [sb(f"{n}_parts", [P, 2, QUAD * P], F32R) for n in "qk"]
        stack = [sb(f"{n}_stack", [P, SLOTS, 4, T], F32R) for n in "qk"]
        vaug = sb("vaug", [P, SLOTS, QT, H, V1])
        mraw = sb("mraw", [P, QT, GRP])
        mhl = sb("mhl", [P, QT, 2, GRP], F32R)
        mT = sb("mT", [P, 2, P], F32R)
        pT = sb("pT", [P, 2, 3, GRP, P])
        rl = sb("rl", [P, QT * H])
        yn = sb("yn", [P, QT, C])
        yT = sb("yT", [P, QT * P])
        a_resi = sb("a_resi", [P, QUAD * TOPK], I32)
        spare = sb("spare", [P, 1])
        yg = sb("yg", [P, 2, QUAD * TOPK, C])
        a_yg = yg[:, 0, :, :]
        resg = sb("resg", [P, 2, QUAD * TOPK], I32)

        s_const = sem("s_const")
        s_wexp = sem("s_wexp")
        s_x = [sem(f"s_x{i}") for i in range(NQ)]
        s_bias3 = sem("s_bias3")
        s_setup = sem("s_setup")
        s_vec = sem("s_vec")
        s_act = sem("s_act")
        s_pool = sem("s_pool")
        s_veps = sem("s_veps")
        s_rstd = sem("s_rstd")
        s_xn = sem("s_xn")
        s_xnTp = sem("s_xnTp")
        s_xnT = sem("s_xnT")
        s_logit = sem("s_logit")
        s_mask = sem("s_mask")
        s_rank = sem("s_rank")
        s_pos = sem("s_pos")
        s_scat = sem("s_scat")
        s_count = sem("s_count")
        s_ntile = sem("s_ntile")
        s_cum = sem("s_cum")
        s_table = sem("s_table")
        s_tab = sem("s_tab")
        s_zero = sem("s_zero")
        s_resi = sem("s_resi")
        s_wts = sem("s_wts")
        s_xt = [sem(f"s_xt{i}") for i in range(UNROLL)]
        s_xTp = sem("s_xTp")
        s_xT = sem("s_xT")
        s_gu = sem("s_gu")
        s_sig = sem("s_sig")
        s_gated = sem("s_gated")
        s_gTp = sem("s_gTp")
        s_gT = sem("s_gT")
        s_y = sem("s_y")
        s_ysb = sem("s_ysb")
        s_store = [sem(f"s_store{i}") for i in range(2)]
        s_resg = [sem(f"s_resg{i}") for i in range(2)]
        s_got = [sem(f"s_got{i}") for i in range(2)]
        s_comb = sem("s_comb")
        s_out = sem("s_out")
        s_watt = sem("s_watt")
        s_asetup = sem("s_asetup")
        a_resg = sem("a_resg")
        a_got = sem("a_got")
        a_veps = sem("a_veps")
        a_rstd = sem("a_rstd")
        a_xn = sem("a_xn")
        a_Tp = sem("a_Tp")
        a_xT = sem("a_xT")
        a_q = sem("a_q")
        a_qh = sem("a_qh")
        a_ql = sem("a_ql")
        a_k = sem("a_k")
        a_kh = sem("a_kh")
        a_kl = sem("a_kl")
        a_v = sem("a_v")
        a_vs = sem("a_vs")
        a_s = sem("a_s")
        a_max = sem("a_max")
        a_mTp = sem("a_mTp")
        a_mT = sem("a_mT")
        a_st = sem("a_st")
        a_exp = sem("a_exp")
        a_pv = sem("a_pv")
        a_yn = sem("a_yn")
        a_yTp = sem("a_yTp")
        a_yT = sem("a_yT")
        a_proj = sem("a_proj")
        a_x2 = sem("a_x2")
        a_stack = [sem(f"a_stack{i}") for i in range(2)]

        x_t = x.rearrange("(n p) c -> p n c", p=P)
        out_t = out.rearrange("(n p) c -> p n c", p=P)
        PAIRS = TILES // 2

        block = ctx.enter_context(nc.Block())

        def stack_all(sp):
            def stack_pair(turn, half):
                x = turn * 2 + half
                for which, ready in ((0, a_ql), (1, a_kl)):
                    sp.wait_ge(ready, x + 1)
                    if which == 0:
                        beyond_first(sp, a_st, x * 8 - 8)
                    for g in range(4):
                        for a in range(2):
                            for b in range(2):
                                p = 2 * a + b if which == 0 else 2 * b + a
                                sp.dma_start(stack[which][p:P:4, 2 * half:2 * half + 2, g, :].bitcast(F32),
                                             hl[which][32 * g:32 * g + 32, a, :].rearrange("p (s t) -> p s t", s=2).bitcast(F32),
                                             ).then_inc(a_stack[half], 16)

            for half in range(2):
                stack_pair(0, half)
            with sp.Fori(1, TURNS_A) as t:
                for half in range(2):
                    stack_pair(t, half)

        @block.sync
        def _(sp):
            sp.dma_start(kc[:, :], konst).then_inc(s_const, 16)
            sp.dma_start(xr[:, 0:QUAD, :], x_t[:, 0:QUAD, :]).then_inc(s_x[0], 16)
            sp.dma_start(wg[:, :], w_g).then_inc(s_const, 16)
            sp.dma_start(bg[:, :], b_g.partition_broadcast(P)).then_inc(s_const, 16)
            for q in range(1, NQ):
                sp.dma_start(xr[:, QUAD * q:QUAD * q + QUAD, :], x_t[:, QUAD * q:QUAD * q + QUAD, :]).then_inc(s_x[q], 16)
            sp.dma_start(bias_in[0:E, 0:2 * F], b_gu).then_inc(s_bias3, 16)
            sp.dma_start(bias_in[0:E, 2 * F:EW], b_d).then_inc(s_bias3, 16)
            sp.dma_start(bias_in[E:NB, 0:C], b_attn[2:3, :]).then_inc(s_bias3, 16)
            sp.dma_start(bias_in[E:NB, C:2 * C], b_proj).then_inc(s_bias3, 16)
            sp.dma_start(bias_in[E:NB, 2 * C:EW], b_proj).then_inc(s_bias3, 16)
            sp.dma_start(wgu[:, :], w_gu).then_inc(s_wexp, 16)
            sp.dma_start(wd[:, :], w_d).then_inc(s_wexp, 16)
            sp.wait_ge(s_setup, 2)
            for r, part in enumerate((bias_hi, bias_mid, bias_lo)):
                sp.dma_start(bias3[r:r + 1, :].rearrange("a (e w) -> a e w", e=NB), part[:, :]).then_inc(s_bias3, 16)

            sp.dma_start(w_in[:, :], w_attn).then_inc(s_watt, 16)
            sp.dma_start(w_out[:, :], w_proj).then_inc(s_watt, 16)
            for i in range(2):
                sp.dma_start(bqk[:, i:i + 1], b_attn[i:i + 1, :].rearrange("a c -> c a")).then_inc(s_watt, 16)

            for f in range(2):
                if f == 1:
                    stack_all(sp)
                sp.wait_ge(s_table, 1 + f)
                for k in range(2):
                    sp.dma_start(tab[0:1, k * TILES:(k + 1) * TILES], tabc[0:TILES, k:k + 1]).then_inc(s_tab, 16)
                sp.dma_start(tab[0:1, 2 * TILES:2 * TILES + E], zrow[:, :]).then_inc(s_tab, 16)
                sp.wait_ge(s_tab, 48 * (f + 1))
                with sp.Fori(0, E) as e:
                    r = sp.value_load(tab[0:1, bass.ds(e + 2 * TILES, 1)], min_val=0, max_val=E * REGION - P)
                    sp.dma_start(rows_dram[bass.ds(r, P), :], zeros[:, :]).then_inc(s_zero, 16)
                sp.wait_ge(s_zero, 16 * E * (f + 1))
                sp.wait_ge(s_scat, 16 * NT * TOPK * (f + 1))

                def load_tile(turn, u):
                    r = sp.value_load(tab[0:1, bass.ds(turn * UNROLL + (TILES + u), 1)], min_val=0, max_val=E * REGION - P)
                    sp.dma_start(xt[:, u, :], rows_dram[bass.ds(r, P), :]).then_inc(s_xt[u], 16)

                for u in range(UNROLL):
                    load_tile(0, u)
                with sp.Fori(1, TURNS) as t:
                    for k in range(2):
                        sp.wait_ge(s_xTp, t * 2 + (k - 1) + f * PAIRS)
                        for u in (2 * k, 2 * k + 1):
                            load_tile(t, u)
            for q in range(NQ):
                sp.wait_ge(s_comb, q + 1)
                sp.dma_start(out_t[:, QUAD * q:QUAD * q + QUAD, :], xr[:, QUAD * q:QUAD * q + QUAD, :]).then_inc(s_out, 16)
            sp.wait_ge(s_out, 16 * NQ)

        @block.gpsimd
        def _(pool):
            nc.gpsimd.memset(zeros[:, :], 0.0).then_inc(s_pool, 1)
            nc.gpsimd.memset(neghalf[:, :], -0.5).then_inc(s_pool, 1)
            pool.wait_ge(s_pool, 2)
            for f in range(2):
                if f == 1:
                    with pool.Fori(1, B // 2 + 1) as x:
                        pool.wait_ge(s_pool, 2)
                        pool.wait_ge(a_resg, x)
                        for c in range(QUAD * TOPK):
                            pool.indirect_dma_start(
                                out=a_yg[:, c, :], out_offset=None, in_=results_dram,
                                in_offset=bass.IndirectOffsetOnAxis(ap=a_resi[:, c:c + 1], axis=0)).then_inc(a_got, 16)
                        pool.wait_ge(a_veps, x)
                        nc.gpsimd.tensor_tensor(a_rs[:, :], a_ve[:, :], neghalf[:, :], ALU.pow).then_inc(a_rstd, 1)

                def root(q):
                    pool.wait_ge(s_veps, f * NQ + q + 1)
                    nc.gpsimd.tensor_tensor(rstd[:, QUAD * q:QUAD * q + QUAD], veps[:, QUAD * q:QUAD * q + QUAD],
                                            neghalf[:, :], ALU.pow).then_inc(s_rstd, 1)

                def scatter(q):
                    pool.wait_ge(s_pos, f * NQ + q + 1)
                    for i in range(QUAD):
                        t = QUAD * q + i
                        for k in range(TOPK):
                            c = t * TOPK + k
                            pool.indirect_dma_start(
                                out=rows_dram, out_offset=bass.IndirectOffsetOnAxis(ap=posi[:, c:c + 1], axis=0),
                                in_=xn[:, t, :], in_offset=None).then_inc(s_scat, 16)

                for q in range(NQ + 3):
                    if q < NQ:
                        root(q)
                    if q >= 3:
                        scatter(q - 3)

                with pool.Fori(0, TURNS) as t:
                    for k in range(2):
                        pool.wait_ge(s_ysb, t * 2 + (k + 1 + f * PAIRS))
                        pool.dma_start(results_dram[bass.ds((t * 2 + k) * (2 * P), 2 * P), :].rearrange("(n p) c -> p n c", p=P),
                                       ysb[:, k, :, :]).then_inc(s_store[k], 16)

                for k in range(2):
                    pool.wait_ge(s_store[k], 16 * TURNS * (f + 1))
            with pool.Fori(1, NQ // 2 + 1) as h:
                for u in range(2):
                    pool.wait_ge(s_pool, 2)
                    pool.wait_ge(s_resg[u], h)
                    for c in range(QUAD * TOPK):
                        pool.indirect_dma_start(
                            out=yg[:, u, c, :], out_offset=None, in_=results_dram,
                            in_offset=bass.IndirectOffsetOnAxis(ap=resg[:, u, c:c + 1], axis=0)).then_inc(s_got[u], 16)

        def attention_scalar(act):
            def evac_xT(x):
                act.wait_ge(a_Tp, x + 1)
                nc.scalar.activation(xaT[:, :], bank[7][:, :], ACT.Identity).then_inc(a_xT, 1)

            def high(which, x, made, done, slot_done):
                act.wait_ge(made, x + 1)
                slot_done(act, x)
                nc.scalar.activation(hl[which][:, 0, :], bank[7][:, :], ACT.Identity, bias=bqk[:, which:which + 1]).then_inc(done, 1)

            def evac_v(x, half):
                act.wait_ge(a_v, x + 1)
                nc.scalar.activation(vaug[:, 2 * half:2 * half + 2, :, :, 0:D].rearrange("p s k h d -> p (s k) h d"),
                                     bank[7][:, :].rearrange("p (n h d) -> p n h d", n=QUAD, h=H), ACT.Identity).then_inc(a_vs, 1)

            def evac_max(t, s):
                n = t * UNITS + s
                act.wait_ge(a_mTp, n + 1)
                beyond_first(act, a_st, n - 1)
                nc.scalar.activation(mT[0:2 * QT * GRP, s % 2, :], bank[7][0:2 * QT * GRP, 0:P], ACT.Identity, scale=-1.0).then_inc(a_mT, 1)

            def exp(t, s):
                n = t * UNITS + s
                act.wait_ge(a_st, n + 1)
                nc.scalar.activation(pT[:, s % 2, :, :, :].rearrange("p a g q -> p (a g q)"),
                                     banks[:, 3:6, :].rearrange("p a q -> p (a q)"), ACT.Exp, scale=SCALE).then_inc(a_exp, 1)

            def evac_yT(b):
                act.wait_ge(a_yTp, b + 2)
                nc.scalar.activation(yT[:, :], bank[7][:, 0:QT * P], ACT.Identity).then_inc(a_yT, 1)

            def stacked(eng, x, turn, half):
                beyond_first(eng, a_stack[1 - half], (turn if half == 0 else turn + 1) * STACKED)

            def qk(which, x, turn, half):
                high(which, x, (a_q, a_k)[which], (a_qh, a_kh)[which], lambda eng, _: stacked(eng, x, turn, half))

            evac_xT(0)
            qk(0, 0, 0, 0)
            qk(1, 0, 0, 0)
            evac_v(0, 0)
            evac_xT(1)
            evac_max(0, 0)

            def unit(t, s):
                v, j = s // GRP % SLOTS, s % GRP
                t, s = t + s // UNITS, s % UNITS
                steps = attention_steps(t, s)
                if steps.max_next:
                    evac_max(*after(t, s, 1))
                exp(t, s)
                if steps.q is not None:
                    qk(0, steps.q, *steps.pair)
                if steps.k is not None:
                    qk(1, steps.k, *steps.pair)
                if steps.v is not None:
                    evac_v(steps.v, steps.pair[1])
                if steps.x is not None:
                    evac_xT(steps.x)
                if steps.y is not None:
                    evac_yT(steps.y)

            attention_loop(act, unit, None)
            evac_yT(B - 1)

        @block.scalar
        def _(act):
            for f in range(2):
                if f == 1:
                    attention_scalar(act)
                for q in range(NQ):
                    act.wait_ge(s_xnTp, f * NQ + q + 1)
                    if q >= 2:
                        act.wait_ge(s_logit, f * NQ + q - 1)
                    nc.scalar.activation(xnT[:, q % 2, :], bank[q % 2][:, :], ACT.Identity).then_inc(s_xnT, 1)
                act.wait_ge(s_mask, (f + 1) * NQ)
                nc.scalar.activation(wts[:, 0, :], gap[:, :], ACT.Sigmoid).then_inc(s_wts, 1)
                nc.scalar.activation(wts[:, 1, :], gap[:, :], ACT.Sigmoid, scale=-1.0).then_inc(s_wts, 1)

                def evac_x(t, k):
                    n = t * 2 + k + f * PAIRS
                    act.wait_ge(s_xTp, n + 1)
                    nc.scalar.activation(xT[:, k, :], bank[k][:, 0:2 * P], ACT.Identity).then_inc(s_xT, 1)

                def sigmoid(t, k):
                    n = t * 2 + k + f * PAIRS
                    act.wait_ge(s_gu, n + 1)
                    nc.scalar.activation(sig[:, k, :, :], bank[2 + k][:, :].rearrange("p (n w) -> p n w", n=2)[:, :, 0:F],
                                         ACT.Sigmoid, scale=ALPHA).then_inc(s_sig, 1)

                def evac_g(t, k):
                    n = t * 2 + k + f * PAIRS
                    act.wait_ge(s_gTp, n + 1)
                    nc.scalar.activation(gT[:, k, :], bank[4 + k][:, 0:2 * P], ACT.Identity).then_inc(s_gT, 1)

                def evac_y(t, k):
                    n = t * 2 + k + f * PAIRS
                    act.wait_ge(s_y, n + 1)
                    beyond_first(act, s_store[k], (t + f * TURNS) * 16)
                    nc.scalar.activation(ysb[:, k, :, :].rearrange("p n c -> p (n c)"), bank[6 + k][:, 0:2 * P],
                                         ACT.Identity).then_inc(s_ysb, 1)

                expert_pipeline(act, evac_x, sigmoid, evac_g, evac_y)

        def attention_vector(dve, ch):
            def name_rows(x):
                nc.vector.tensor_copy(a_resi[:, :], resi[:, bass.ds(x * (QUAD * TOPK), QUAD * TOPK)]).then_inc(a_resg, 1)

            def row(x, i):
                return xr[:, bass.ds(x * QUAD + i, 1), :].rearrange("p a c -> p (a c)")

            def combine(x):
                dve.wait_ge(a_got, (x + 1) * (16 * QUAD * TOPK))
                for k in range(TOPK):
                    for i in range(QUAD):
                        ch.mark(nc.vector.scalar_tensor_tensor(out=row(x, i), in0=a_yg[:, TOPK * i + k, :], scalar=wts[:, k, bass.ds(x * QUAD + i, 1)],
                                                               in1=row(x, i), op0=ALU.mult, op1=ALU.add))
                    if k < TOPK - 1:
                        ch.wait()

            def settle():
                ch.wait()
                ch.mark(nc.vector.memset(spare[:, :], 0.0))

            def stats(x):
                settle()
                for i in range(QUAD):
                    ch.mark(nc.vector.bn_stats(a_st6[:, i, :], row(x, i)))
                settle()
                for i in range(QUAD):
                    ch.mark(nc.vector.bn_aggr(a_mv[:, i, :], a_st6[:, i, :]))
                ch.wait()
                nc.vector.tensor_scalar(a_ve[:, :], a_mv[:, :, 1], EPS, None, ALU.add).then_inc(a_veps, 1)

            def normalise(x):
                dve.wait_ge(a_rstd, x + 1)
                beyond_first(dve, a_Tp, x)
                for i in range(QUAD):
                    last = nc.vector.tensor_scalar(xa[:, i, :], row(x, i), a_mv[:, i, 0:1], a_rs[:, i:i + 1], ALU.subtract, ALU.mult)
                last.then_inc(a_xn, 1)

            def low(which, x):
                high, done = ((a_qh, a_ql), (a_kh, a_kl))[which]
                dve.wait_ge(high, x + 1)
                nc.vector.scalar_tensor_tensor(out=hl[which][:, 1, :], in0=bank[7][:, :], scalar=bqk[:, which:which + 1],
                                               in1=hl[which][:, 0, :].bitcast(F32), op0=ALU.add, op1=ALU.subtract).then_inc(done, 1)

            def row_max(t, s):
                n = t * UNITS + s
                dve.wait_ge(a_s, n + 1)
                beyond_first(dve, a_mTp, n)
                ch.mark(nc.vector.tensor_reduce(mraw[:, 0, :], bank[0][:, :].rearrange("p (g k) -> p g k", g=GRP), AX.X, ALU.max))
                ch.mark(nc.vector.tensor_reduce(mraw[:, 1, :], banks[:, 1:3, :].rearrange("p a (g k) -> p g a k", g=GRP), AX.XY, ALU.max))
                ch.wait()
                ch.mark(nc.vector.tensor_copy(mhl[:, :, 0, :], mraw[:, :, :]))
                ch.wait()
                nc.vector.tensor_tensor(mhl[:, :, 1, :], mraw[:, :, :], mhl[:, :, 0, :].bitcast(F32), ALU.subtract).then_inc(a_max, 1)

            def divide(b):
                dve.wait_ge(a_pv, (b + 1) * GRP)
                dve.wait_ge(a_yTp, b + 1)
                pv = bank[6][:, 0:QT * H * V1].rearrange("p (h d) -> p h d", d=V1)
                ch.mark(nc.vector.reciprocal(rl[:, :], pv[:, :, D]))
                ch.wait()
                nc.vector.tensor_tensor(yn[:, :, :].rearrange("p n (h d) -> p (n h) d", d=D), pv[:, :, 0:D],
                                        rl[:, :].unsqueeze(2).to_broadcast([P, QT * H, D]), ALU.mult).then_inc(a_yn, 1)

            def add_attention(b):
                dve.wait_ge(a_proj, b + 2)
                rows = xs[:, bass.ds((b + 1) * QT, QT), :].rearrange("p n c -> p (n c)")
                nc.vector.tensor_tensor(rows, bank[7][:, 0:QT * C], rows, ALU.add).then_inc(a_x2, 1)

            name_rows(0)
            for x in range(2):
                combine(x)
                if x == 0:
                    name_rows(1)
                stats(x)
                normalise(x)
                if x == 0:
                    low(0, 0)
                    low(1, 0)
            row_max(0, 0)
            row_max(0, 1)

            def unit(t, s):
                t, s = t + s // UNITS, s % UNITS
                steps = attention_steps(t, s)
                if steps.scores_next:
                    row_max(*after(t, s, 2))
                if steps.q is not None:
                    low(0, steps.q)
                if steps.k is not None:
                    low(1, steps.k)
                if steps.divide is not None:
                    divide(steps.divide)
                if steps.add is not None:
                    add_attention(steps.add)
                if steps.name is not None:
                    name_rows(steps.name)
                if steps.combine is not None:
                    combine(steps.combine)
                    stats(steps.combine)
                if steps.normalise is not None:
                    normalise(steps.normalise)

            attention_loop(dve, unit, (ch, ATT_CHAIN))
            divide(B - 1)
            add_attention(B - 1)

        @block.vector
        def _(dve):
            ch = Chain(dve, s_vec)
            dve.wait_ge(s_const, 48)
            nc.vector.tensor_copy(tri[:, :], kc[:, K_TRI:K_TRI + P]).then_inc(s_setup, 1)
            ch.mark(nc.vector.memset(ones[:, :], 1.0))
            ch.mark(nc.vector.tensor_copy(utri[:, :], kc[0:E, K_U:K_U + 2 * E]))
            ch.mark(nc.vector.memset(macc[:, :, :], 0.0))

            nc.vector.tensor_copy(identb[:, :], ident).then_inc(s_asetup, 1)
            nc.vector.tensor_copy(mask_q[:, :], kc[:, K_MQ:K_MQ + P]).then_inc(s_asetup, 1)
            nc.vector.tensor_copy(mask_k[:, :], kc[:, K_MK:K_MK + P]).then_inc(s_asetup, 1)
            nc.vector.memset(vaug[:, :, :, :, :], 1.0).then_inc(s_asetup, 1)
            nc.vector.memset(yn[:, :, :], 0.0).then_inc(a_yn, 1)
            nc.vector.memset(xs[:, 0:QT, :], 0.0).then_inc(s_asetup, 1)
            nc.vector.memset(mT[:, :, :].bitcast(F32), 0.0).then_inc(s_asetup, 1)
            nc.vector.tensor_copy(select[:, :, :].rearrange("p a k -> p (a k)"), kc[:, K_SEL:K_SEL + 8 * P]).then_inc(s_asetup, 1)

            for f in range(2):
                if f == 1:
                    attention_vector(dve, ch)

                def stats(q):
                    if f == 0:
                        dve.wait_ge(s_x[q], 16)
                    for t in range(QUAD * q, QUAD * q + QUAD):
                        ch.mark(nc.vector.bn_stats(st6[:, t, :], xr[:, t, :]))
                    ch.wait()
                    for t in range(QUAD * q, QUAD * q + QUAD):
                        ch.mark(nc.vector.bn_aggr(mv[:, t, :], st6[:, t, :]))
                    ch.wait()
                    nc.vector.tensor_scalar(veps[:, QUAD * q:QUAD * q + QUAD], mv[:, QUAD * q:QUAD * q + QUAD, 1],
                                            EPS, None, ALU.add).then_inc(s_veps, 1)

                def normalise(q):
                    dve.wait_ge(s_rstd, f * NQ + q + 1)
                    for t in range(QUAD * q, QUAD * q + QUAD):
                        last = nc.vector.tensor_scalar(xn[:, t, :], xr[:, t, :], mv[:, t, 0:1], rstd[:, t:t + 1],
                                                       ALU.subtract, ALU.mult)
                    last.then_inc(s_xn, 1)

                def top2(q):
                    ts = slice(QUAD * q, QUAD * q + QUAD)
                    dve.wait_ge(s_logit, f * NQ + q + 1)
                    ch.mark(nc.vector.tensor_tensor(lg[:, q, :, :], bank[2 + q % 2][:, 0:QUAD * E].rearrange("p (n e) -> p n e", n=QUAD),
                                                    bg[:, :].unsqueeze(1).to_broadcast([P, QUAD, E]), ALU.add))
                    ch.wait()
                    for i in range(QUAD):
                        ch.mark(nc.vector.max(mx[:, QUAD * q + i, :], lg[:, q, i, :]))
                    ch.wait()
                    for i in range(QUAD):
                        ch.mark(nc.vector.max_index(mi[:, QUAD * q + i, :], mx[:, QUAD * q + i, :], lg[:, q, i, :]))
                    ch.mark(nc.vector.tensor_tensor(gap[:, ts], mx[:, ts, 0], mx[:, ts, 1], ALU.subtract))
                    ch.wait()
                    ch.mark(nc.vector.tensor_copy(mif[:, ts, :], mi[:, ts, 0:TOPK]))
                    ch.wait()
                    ch.mark(nc.vector.tensor_tensor(
                        oh[:, ts, :, :].rearrange("p n k e -> p (n k) e"),
                        kc[:, K_E:K_E + E].unsqueeze(1).to_broadcast([P, QUAD * TOPK, E]),
                        mif[:, ts, :].rearrange("p n k -> p (n k)").unsqueeze(2).to_broadcast([P, QUAD * TOPK, E]), ALU.is_equal))
                    ch.wait()
                    ch.mark(nc.vector.tensor_tensor(mask[:, ts, :], oh[:, ts, 0, :], oh[:, ts, 1, :], ALU.add))
                    ch.wait()
                    ch.mark(nc.vector.tensor_reduce(msum[:, q, :], mask[:, ts, :].rearrange("p n e -> p e n"), AX.X, ALU.add))
                    ch.wait()
                    nc.vector.tensor_tensor(macc[:, q + 1, :], macc[:, q, :], msum[:, q, :], ALU.add).then_inc(s_mask, 1)

                def positions(q):
                    dve.wait_ge(s_rank, f * NQ + q + 1)
                    ch.mark(nc.vector.tensor_tensor(rank[:, q, :, :], bank[4 + q % 2][:, 0:QUAD * E].rearrange("p (n e) -> p n e", n=QUAD),
                                                    kc[:, K_BASE:K_BASE + E].unsqueeze(1).to_broadcast([P, QUAD, E]), ALU.add))
                    ch.wait()
                    for k in range(TOPK):
                        ch.mark(nc.vector.tensor_tensor(
                            rsel[:, q, :, :].rearrange("p (n k) e -> p n k e", k=TOPK)[:, :, k, :],
                            oh[:, QUAD * q:QUAD * q + QUAD, k, :], rank[:, q, :, :], ALU.mult))
                    ch.wait()
                    cs = slice(QUAD * TOPK * q, QUAD * TOPK * (q + 1))
                    ch.mark(nc.vector.tensor_reduce(posf[:, cs], rsel[:, q, :, :], AX.X, ALU.add))
                    ch.wait()
                    nc.vector.tensor_copy(posi[:, cs], posf[:, cs]).then_inc(s_pos, 1)

                def split_biases():
                    dve.wait_ge(s_bias3, 80)
                    ch.mark(nc.vector.tensor_copy(bias_hi[:, :], bias_in[:, :]))
                    ch.wait()
                    ch.mark(nc.vector.tensor_tensor(bias_r1[:, :], bias_in[:, :], bias_hi[:, :], ALU.subtract))
                    ch.wait()
                    ch.mark(nc.vector.tensor_copy(bias_mid[:, :], bias_r1[:, :]))
                    ch.wait()
                    ch.mark(nc.vector.tensor_tensor(bias_r2[:, :], bias_r1[:, :], bias_mid[:, :], ALU.subtract))
                    ch.wait()
                    nc.vector.tensor_copy(bias_lo[:, :], bias_r2[:, :]).then_inc(s_setup, 1)

                for q in range(NQ + 2):
                    if 1 <= q <= NQ:
                        top2(q - 1)
                    if q < NQ:
                        stats(q)
                    if 2 <= q:
                        positions(q - 2)
                    if q < NQ:
                        normalise(q)
                    if f == 0 and q == 2:
                        split_biases()
                dve.wait_ge(s_count, f + 1)
                ch.mark(nc.vector.tensor_scalar(cnt[:, :], bank[6][0:E, 0:P], 1.0 / P, (P - 1.0) / P - 0.5 + 0.5 / P, ALU.mult, ALU.add))
                ch.wait()
                ch.mark(nc.vector.tensor_scalar(cntr[:, :], cnt[:, :], ROUND, None, ALU.add))
                ch.wait()
                nc.vector.tensor_scalar(ntile[:, :], cntr[:, :], -ROUND, None, ALU.add).then_inc(s_ntile, 1)
                ch.mark(nc.vector.tensor_scalar(zrow[:, :], bank[6][0:E, 0:1], kc[0:E, K_BASEP:K_BASEP + 1], None, ALU.add))
                dve.wait_ge(s_cum, f + 1)
                ch.mark(nc.vector.tensor_copy(cum[:, :], bank[7][:, 0:2 * E]))
                ch.wait()
                ch.mark(nc.vector.scalar_tensor_tensor(out=delta[:, :], in0=cum[:, E:2 * E], scalar=float(P),
                                                       in1=kc[:, K_BASE:K_BASE + E], op0=ALU.mult, op1=ALU.subtract))
                ch.mark(nc.vector.tensor_scalar(below[:, :], cum[:, :], kc[:, K_ROW:K_ROW + 1], None, ALU.is_le))
                ch.wait()
                ch.mark(nc.vector.tensor_tensor(hot[:, :], below[:, E:2 * E], below[:, 0:E], ALU.subtract))
                ch.mark(nc.vector.tensor_scalar(rowof[:, :], delta[:, :], -1.0, kc[:, K_ROW128:K_ROW128 + 1], ALU.mult, ALU.add))
                ch.wait()
                ch.mark(nc.vector.tensor_tensor(tmp2[:, 0, :], hot[:, :], kc[:, K_E:K_E + E], ALU.mult))
                ch.mark(nc.vector.tensor_tensor(tmp2[:, 1, :], hot[:, :], rowof[:, :], ALU.mult))
                ch.wait()
                ch.mark(nc.vector.tensor_reduce(tabf[:, :], tmp2[:, :, :], AX.X, ALU.add))
                ch.wait()
                nc.vector.tensor_copy(tabc[:, :], tabf[:, :]).then_inc(s_table, 1)
                ch.mark(nc.vector.tensor_tensor(dsel[:, :, :], oh[:, :, :, :].rearrange("p n k e -> p (n k) e"),
                                                delta[:, :].unsqueeze(1).to_broadcast([P, NT * TOPK, E]), ALU.mult))
                ch.wait()
                ch.mark(nc.vector.tensor_reduce(dsum[:, :], dsel[:, :, :], AX.X, ALU.add))
                ch.wait()
                ch.mark(nc.vector.tensor_tensor(resi[:, :], dsum[:, :], posf[:, :], ALU.add))
                dve.wait_ge(s_wts, 2 * (f + 1))
                ch.mark(nc.vector.tensor_scalar(wts[:, :, :], wts[:, :, :], 0.5, None, ALU.mult))
                ch.wait()

                def gate(t, k):
                    n = t * 2 + k + f * PAIRS
                    dve.wait_ge(s_sig, n + 1)
                    gu = bank[2 + k][:, :].rearrange("p (n w) -> p n w", n=2)
                    ch.mark(nc.vector.scalar_tensor_tensor(out=glu[:, k, :, :], in0=gu[:, :, 0:F], scalar=LIMIT,
                                                           in1=sig[:, k, :, :], op0=ALU.min, op1=ALU.mult))
                    ch.mark(nc.vector.tensor_scalar(upc[:, k, :, :], gu[:, :, F:2 * F], LIMIT, -LIMIT, ALU.min, ALU.max))
                    ch.wait()
                    nc.vector.scalar_tensor_tensor(out=gated[:, k, :, :], in0=upc[:, k, :, :], scalar=1.0,
                                                   in1=glu[:, k, :, :], op0=ALU.add, op1=ALU.mult).then_inc(s_gated, 1)

                ch.begin(0, 4)
                for k in range(2):
                    gate(0, k)
                ch.end(1)
                with dve.Fori(1, TURNS) as t:
                    ch.begin(t - 1, 4)
                    for k in range(2):
                        gate(t, k)
                ch.end(TURNS - 1)
                if f == 0:
                    continue

                def stage_rows(h, u):
                    nc.vector.tensor_copy(resg[:, u, :], resi[:, bass.ds((h * 2 + u) * (QUAD * TOPK), QUAD * TOPK)]).then_inc(s_resg[u], 1)

                def combine(h, u):
                    dve.wait_ge(s_got[u], (h + 1) * (16 * QUAD * TOPK))
                    for k in range(TOPK):
                        for i in range(QUAD):
                            t = h * (2 * QUAD) + (u * QUAD + i)
                            row = xr[:, bass.ds(t, 1), :].rearrange("p a c -> p (a c)")
                            ins = nc.vector.scalar_tensor_tensor(out=row, in0=yg[:, u, TOPK * i + k, :], scalar=wts[:, k, bass.ds(t, 1)],
                                                                 in1=row, op0=ALU.mult, op1=ALU.add)
                            if k < TOPK - 1:
                                ch.mark(ins)
                        if k < TOPK - 1:
                            ch.wait()
                    ins.then_inc(s_comb, 1)

                for u in range(2):
                    stage_rows(0, u)
                with dve.Fori(0, NQ // 2 - 1) as h:
                    ch.begin(h, 2 * QUAD)
                    for u in range(2):
                        combine(h, u)
                        stage_rows(h + 1, u)
                ch.end(NQ // 2 - 1)
                for u in range(2):
                    combine(NQ // 2 - 1, u)

        def attention_tensor(pe):
            pe.wait_ge(s_watt, 64)
            pe.wait_ge(s_asetup, 7)

            def rows_T(x):
                pe.wait_ge(a_xn, x + 1)
                for i in range(QUAD):
                    last = nc.tensor.transpose(bank[7][:, i * P:(i + 1) * P], xa[:, i, :], ident)
                last.then_inc(a_Tp, 1)

            def project(which, x):
                if which == 0:
                    pe.wait_ge(a_xT, x + 1)
                nc.tensor.matmul(bank[7][:, :], w_in[:, which * C:(which + 1) * C], xaT[:, :], start=True, stop=True).then_inc((a_q, a_k)[which], 1)

            def values(x):
                for i in range(QUAD):
                    o = bank[7][:, i * C:(i + 1) * C]
                    nc.tensor.matmul(o, ones[0:3, :], bias3[:, E * EW:E * EW + C], start=True, stop=False)
                    last = nc.tensor.matmul(o, xaT[:, i * P:(i + 1) * P], w_in[:, 2 * C:3 * C], start=False, stop=True)
                last.then_inc(a_v, 1)

            def scores(t, s):
                n, v, j = t * UNITS + s, s // GRP, s % GRP
                if j == 0 and v % 2 == 0:
                    pe.wait_ge(a_stack[v // 2], (t + 1) * STACKED)
                beyond_first(pe, a_max, n)
                r = slice(32 * j, 32 * j + 32)
                q, k = stack
                for blk, qt, kt in ((0, 0, 0), (1, 1, 0), (2, 1, 1)):
                    o = bank[blk][:, :]
                    if qt == kt:
                        nc.tensor.matmul(o.rearrange("p (g k) -> p g k", g=GRP), identb[:, :],
                                         mask_q[:, :].unsqueeze(1).to_broadcast([P, GRP, P]), start=True, stop=False)
                    for g in range(GRP):
                        last = nc.tensor.matmul(o[:, g * P:(g + 1) * P], q[r, v, g, qt * P:(qt + 1) * P], k[r, v, g, kt * P:(kt + 1) * P],
                                                start=qt != kt, stop=g == GRP - 1 or qt != kt)
                last.then_inc(a_s, 1)

            def max_T(t, s):
                n = t * UNITS + s
                pe.wait_ge(a_max, n + 1)
                nc.tensor.transpose(bank[7][0:2 * QT * GRP, 0:P], mhl[:, :, :, :].rearrange("p a b g -> p (a b g)").bitcast(F32),
                                    ident).then_inc(a_mTp, 1)

            def weights(t, s):
                n, v, j = t * UNITS + s, s // GRP, s % GRP
                pe.wait_ge(a_mT, n + 1)
                beyond_first(pe, a_exp, n)
                r = slice(32 * j, 32 * j + 32)
                q, k = stack
                for blk, qt, kt in ((0, 0, 0), (1, 1, 0), (2, 1, 1)):
                    o = bank[3 + blk][:, :]
                    if qt == kt:
                        nc.tensor.matmul(o.rearrange("p (g k) -> p g k", g=GRP), identb[:, :],
                                         mask_k[:, :].unsqueeze(1).to_broadcast([P, GRP, P]), start=True, stop=False)
                    for g in range(GRP):
                        nc.tensor.matmul(o[:, g * P:(g + 1) * P], select[:, qt * GRP + g, :], mT[:, s % 2, :],
                                         start=qt != kt and g == 0, stop=False)
                    for g in range(GRP):
                        last = nc.tensor.matmul(o[:, g * P:(g + 1) * P], k[r, v, g, kt * P:(kt + 1) * P], q[r, v, g, qt * P:(qt + 1) * P],
                                                start=False, stop=g == GRP - 1)
                last.then_inc(a_st, 1)

            def weigh_values(t, s):
                n, v, j = t * UNITS + s, s // GRP, s % GRP
                pe.wait_ge(a_exp, n + 1)
                if j == 0:
                    b = t * SLOTS + v
                    pe.wait_ge(a_yn, b + 1)
                    if v % 2 == 0:
                        pe.wait_ge(a_vs, t * 2 + (v // 2 + 1))
                for g in range(GRP):
                    h = GRP * g + j
                    for qt in range(QT):
                        o = bank[6][:, (qt * H + h) * V1:(qt * H + h + 1) * V1]
                        for kt in range(qt + 1):
                            last = nc.tensor.matmul(o, pT[:, s % 2, qt + kt, g, :], vaug[:, v, kt, h, :], start=kt == 0, stop=kt == qt)
                last.then_inc(a_pv, 1)

            def turn_y(b):
                pe.wait_ge(a_yn, b + 2)
                for i in range(QT):
                    last = nc.tensor.transpose(bank[7][:, i * P:(i + 1) * P], yn[:, i, :], ident)
                last.then_inc(a_yTp, 1)

            def project_out(b):
                pe.wait_ge(a_yT, b + 2)
                for i in range(QT):
                    o = bank[7][:, i * C:(i + 1) * C]
                    nc.tensor.matmul(o, ones[0:3, :], bias3[:, E * EW + C:E * EW + 2 * C], start=True, stop=False)
                    last = nc.tensor.matmul(o, yT[:, i * P:(i + 1) * P], w_out[:, :], start=False, stop=True)
                last.then_inc(a_proj, 1)

            rows_T(0)
            project(0, 0)
            pe.wait_ge(a_ql, 1)
            project(1, 0)
            pe.wait_ge(a_kl, 1)
            values(0)
            pe.wait_ge(a_vs, 1)
            rows_T(1)
            scores(0, 0)
            scores(0, 1)
            pe.wait_ge(a_xT, 2)
            max_T(0, 0)

            def bank7_read(t, s):
                steps = attention_steps(t, s)
                for step, sem_read in ((steps.q, a_ql), (steps.k, a_kl), (steps.v, a_vs), (steps.x, a_xT)):
                    if step is not None:
                        pe.wait_ge(sem_read, step + 1)
                for step, sem_read in ((steps.y, a_yT), (steps.project, a_x2)):
                    if step is not None:
                        pe.wait_ge(sem_read, step + 2)

            def unit(t, s):
                t0, s0 = t, s
                t, s = t + s // UNITS, s % UNITS
                n = t * UNITS + s
                steps = attention_steps(t, s)
                if steps.scores_next:
                    scores(*after(t, s, 2))
                if steps.max_next:
                    if s0 > 0:
                        bank7_read(*after(t0, s0 - 1, 0))
                    else:
                        pe.wait_ge(a_mT, 1)
                    max_T(*after(t, s, 1))
                weights(t, s)
                if steps.max_next:
                    pe.wait_ge(a_mT, n + 2)
                elif s0 > 0:
                    bank7_read(*after(t0, s0 - 1, 0))
                if steps.q is not None:
                    project(0, steps.q)
                if steps.k is not None:
                    project(1, steps.k)
                if steps.v is not None:
                    values(steps.v)
                if steps.x is not None:
                    rows_T(steps.x)
                if steps.y is not None:
                    turn_y(steps.y)
                if steps.project is not None:
                    project_out(steps.project)
                if s0 > 0:
                    weigh_values(*after(t0, s0 - 1, 0))

            attention_loop(pe, unit, None)
            weigh_values(TURNS_A - 1, UNITS - 1)
            bank7_read(TURNS_A - 1, UNITS - 1)
            turn_y(B - 1)
            project_out(B - 1)

        @block.tensor
        def _(pe):
            pe.wait_ge(s_const, 48)
            for f in range(2):
                if f == 1:
                    attention_tensor(pe)

                def transpose_logits(q):
                    pe.wait_ge(s_xn, f * NQ + q + 1)
                    if q >= 2:
                        pe.wait_ge(s_xnT, f * NQ + q - 1)
                    for i in range(QUAD):
                        last = nc.tensor.transpose(bank[q % 2][:, i * P:(i + 1) * P], xn[:, QUAD * q + i, :], ident)
                    last.then_inc(s_xnTp, 1)
                    pe.wait_ge(s_xnT, f * NQ + q + 1)
                    if q >= 2:
                        pe.wait_ge(s_mask, f * NQ + q - 1)
                    for i in range(QUAD):
                        last = nc.tensor.matmul(bank[2 + q % 2][:, i * E:(i + 1) * E], xnT[:, q % 2, i * P:(i + 1) * P], wg[:, :],
                                                start=True, stop=True)
                    last.then_inc(s_logit, 1)

                def ranks(q):
                    if q == 0 and f == 0:
                        pe.wait_ge(s_setup, 1)
                    pe.wait_ge(s_mask, f * NQ + q + 1)
                    if q >= 2:
                        pe.wait_ge(s_pos, f * NQ + q - 1)
                    o = bank[4 + q % 2][:, 0:QUAD * E]
                    nc.tensor.matmul(o, tri[:, :], mask[:, QUAD * q:QUAD * q + QUAD, :].rearrange("p n e -> p (n e)"), start=True, stop=False)
                    for i in range(QUAD - 1):
                        n = QUAD - 1 - i
                        nc.tensor.matmul(o[:, (i + 1) * E:].rearrange("p (n e) -> p n e", n=n), ones[:, :],
                                         mask[:, QUAD * q + i, :].unsqueeze(1).to_broadcast([P, n, E]), start=False, stop=False)
                    nc.tensor.matmul(o.rearrange("p (n e) -> p n e", n=QUAD), ones[:, :],
                                     macc[:, q, :].unsqueeze(1).to_broadcast([P, QUAD, E]), start=False, stop=True).then_inc(s_rank, 1)

                for q in range(NQ + 1):
                    if q < NQ:
                        transpose_logits(q)
                    if q >= 1:
                        ranks(q - 1)
                nc.tensor.matmul(bank[6][0:E, 0:P], macc[:, NQ, :], ones[:, :], start=True, stop=True).then_inc(s_count, 1)
                pe.wait_ge(s_ntile, f + 1)
                nc.tensor.matmul(bank[7][:, 0:2 * E], ntile[:, :], utri[:, :], start=True, stop=True).then_inc(s_cum, 1)

                pe.wait_ge(s_tab, 48 * (f + 1))
                if f == 0:
                    pe.wait_ge(s_wexp, 32)
                    pe.wait_ge(s_bias3, 80 + 48)

                def expert_of(t, u):
                    return pe.value_load(tab[0:1, bass.ds(t * UNROLL + u, 1)], min_val=0, max_val=E - 1)

                def turn_x(t, k):
                    n = t * 2 + k + f * PAIRS
                    for i in range(2):
                        pe.wait_ge(s_xt[2 * k + i], (t + 1 + f * TURNS) * 16)
                    for i in range(2):
                        last = nc.tensor.transpose(bank[k][:, i * P:(i + 1) * P], xt[:, 2 * k + i, :], ident)
                    last.then_inc(s_xTp, 1)

                def gate_up(t, k):
                    n = t * 2 + k + f * PAIRS
                    e = [expert_of(t, 2 * k + i) for i in range(2)]
                    pe.wait_ge(s_xT, n + 1)
                    for i in range(2):
                        o = bank[2 + k][:, i * 2 * F:(i + 1) * 2 * F]
                        nc.tensor.matmul(o, ones[0:3, :], bias3[:, bass.ds(e[i] * EW, 2 * F)], start=True, stop=False)
                        last = nc.tensor.matmul(o, xT[:, k, i * P:(i + 1) * P], wgu[:, bass.ds(e[i] * (2 * F), 2 * F)],
                                                start=False, stop=True)
                    last.then_inc(s_gu, 1)

                def turn_g(t, k):
                    n = t * 2 + k + f * PAIRS
                    pe.wait_ge(s_gated, n + 1)
                    for i in range(2):
                        last = nc.tensor.transpose(bank[4 + k][:, i * P:(i + 1) * P], gated[:, k, i, :], ident)
                    last.then_inc(s_gTp, 1)

                def down(t, k):
                    n = t * 2 + k + f * PAIRS
                    e = [expert_of(t, 2 * k + i) for i in range(2)]
                    pe.wait_ge(s_gT, n + 1)
                    beyond_first(pe, s_ysb, n - 1)
                    for i in range(2):
                        o = bank[6 + k][:, i * C:(i + 1) * C]
                        nc.tensor.matmul(o, ones[0:3, :], bias3[:, bass.ds(e[i] * EW + 2 * F, C)], start=True, stop=False)
                        last = nc.tensor.matmul(o, gT[:, k, i * P:(i + 1) * P], wd[:, bass.ds(e[i] * C, C)],
                                                start=False, stop=True)
                    last.then_inc(s_y, 1)

                expert_pipeline(pe, turn_x, gate_up, turn_g, down)


class Steps:

    def __init__(self, t, s):
        v, j = s // GRP, s % GRP
        b = t * SLOTS + v
        last = isinstance(t, int) and t == TURNS_A - 1
        half = v // 2

        def pair(ahead):
            x = t * 2 + half + ahead
            return x if not isinstance(x, int) or x < B // 2 else None

        self.scores_next = not last or s + 2 < UNITS
        self.max_next = not last or s + 1 < UNITS
        self.q = self.k = self.v = self.x = self.y = self.project = None
        self.divide = self.add = self.combine = self.name = self.normalise = None
        self.pair = (t, 1) if half == 0 else (t + 1, 0)
        if v % 2 == 0:
            if j == 0:
                self.q = pair(1)
            if j == 1:
                self.k, self.name = pair(1), pair(2)
            if j == 3:
                self.combine = pair(2)
        else:
            if j == 0:
                self.v, self.normalise = pair(1), pair(2)
            if j == 1:
                self.x = pair(2)
        if not isinstance(b, int) or b > 0:
            if j == 0:
                self.divide = b - 1
        if j == 2:
            self.y = b - 1
        if j == 3:
            self.project = self.add = b - 1


def attention_steps(t, s):
    return Steps(t, s)


def after(t, s, ahead):
    return t + (s + ahead) // UNITS, (s + ahead) % UNITS


def attention_loop(eng, unit, chain):
    unit(0, 0)
    with eng.Fori(0, TURNS_A - 1) as t:
        if chain:
            chain[0].begin(t, chain[1])
        for s in range(1, UNITS + 1):
            unit(t, s)
    if chain:
        chain[0].end(TURNS_A - 1)
    for s in range(1, UNITS):
        unit(TURNS_A - 1, s)


ATT_CHAIN = 88


def beyond_first(eng, sem, value):
    if not isinstance(value, int) or value > 0:
        eng.wait_ge(sem, value)


def expert_pipeline(eng, first, second, third, fourth):
    last = TURNS - 1
    first(0, 0)
    first(0, 1)
    second(0, 0)
    first(1, 0)
    second(0, 1)
    third(0, 0)

    def turn(t):
        first(t, 1)
        second(t, 0)
        third(t - 1, 1)
        fourth(t - 1, 0)
        first(t + 1, 0)
        second(t, 1)
        third(t, 0)
        fourth(t - 1, 1)

    turn(1)
    with eng.Fori(2, last) as t:
        turn(t)
    first(last, 1)
    second(last, 0)
    third(last - 1, 1)
    fourth(last - 1, 0)
    second(last, 1)
    third(last, 0)
    fourth(last - 1, 1)
    third(last, 1)
    fourth(last, 0)
    fourth(last, 1)


_OUT = (B, T, C)


def kernel(**inputs):
    import concourse.bacc as bacc
    from concourse.bass_utils import run_bass_kernel_spmd

    w = {k: np.asarray(v) for k, v in inputs.items()}
    parts = {
        "x": w["L0_attn_x"].reshape(N, C),
        "w_g": w["L0_ffn_Wg"].T,
        "b_g": w["L0_ffn_bg"],
        "w_gu": w["L0_ffn_Wgu"].reshape(E, C, F, 2).transpose(1, 0, 3, 2).reshape(C, E * 2 * F),
        "w_d": w["L0_ffn_Wd"].transpose(1, 0, 2).reshape(F, E * C),
        "b_gu": w["L0_ffn_bgu"].reshape(E, F, 2).transpose(0, 2, 1).reshape(E, 2 * F),
        "b_d": w["L0_ffn_bd"],
        "b_attn": w["L0_attn_b_attn"].reshape(3, C),
        "b_proj": w["L0_attn_b_proj"].reshape(1, C),
        "w_attn": w["L0_attn_W_attn"],
        "w_proj": w["L0_attn_W_proj"],
        "konst": shape_constants(),
    }
    nc = bacc.Bacc("TRN2", target_bir_lowering=False, num_devices=1)
    arrays, aps = {}, {}
    for name, a in parts.items():
        arrays[f"in_{name}"] = np.ascontiguousarray(a)
        aps[name] = nc.dram_tensor(f"in_{name}", a.shape, mybir.dt.from_np(a.dtype), kind="ExternalInput").ap()
    out = nc.dram_tensor("out", (N, C), F32, kind="ExternalOutput").ap()
    build_block(nc, out=out, **aps)
    r = run_bass_kernel_spmd(nc, [arrays], core_ids=[0])
    return r.results[0]["out"].reshape(_OUT)
```

```python
from contextlib import ExitStack

import numpy as np

import concourse.bass as bass
from concourse import mybir

F32 = mybir.dt.float32
F32R = mybir.dt.float32r
BF16 = mybir.dt.bfloat16
I32 = mybir.dt.int32
U32 = mybir.dt.uint32
ALU = mybir.AluOpType
ACT = mybir.ActivationFunctionType
AX = mybir.AxisListType

P = 128
B, T, C = 16, 256, 128
N = B * T
NT = N // P
QUAD = 4
NQ = NT // QUAD
E, TOPK, F = 16, 2, 128
REGION = N + P
TILES = N * TOPK // P + E
UNROLL = 8
DUOS = UNROLL // 2
TURNS = TILES // UNROLL
ALPHA, LIMIT, EPS = 1.702, 7.0, 1e-5
ROUND = 1.5 * 2.0 ** 23
EW = 2 * F + C
NEG = -1e30
H, D = 16, 8
SCALE = D ** -0.5
GRP = 4
QT = T // P
HALF = P // 2
PARTS = HALF // D
ROWS_V = HALF + D
SLOTS = 4
UNITS = SLOTS * GRP
TURNS_A = B // SLOTS

K_ID, K_TRI = 0, 128
K_E, K_BASE, K_ROW, K_ROW128, K_BASEP = 256, 272, 288, 289, 290
K_U = 291
K_MQ, K_MK = 323, 451
K_SEL = 579
K_EW = K_SEL + GRP * P
K_W = K_EW + E


def shape_constants():
    p = np.arange(P)
    k = np.zeros((P, K_W), np.float32)
    k[:, K_ID:K_ID + P] = np.eye(P)
    k[:, K_TRI:K_TRI + P] = p[:, None] < p[None, :]
    k[:, K_E:K_E + E] = np.arange(E)
    k[:, K_EW:K_EW + E] = np.arange(E) * EW
    k[:, K_BASE:K_BASE + E] = np.arange(E) * REGION
    k[:, K_ROW] = p
    k[:, K_ROW128] = p * P
    k[:, K_BASEP] = p * REGION
    e = np.arange(E)
    k[:E, K_U:K_U + E] = e[:, None] <= e[None, :]
    k[:E, K_U + E:K_U + 2 * E] = e[:, None] < e[None, :]
    k[:, K_MQ:K_MQ + P] = np.where(p[None, :] > p[:, None], NEG, 0)
    k[:, K_MK:K_MK + P] = np.where(p[:, None] > p[None, :], NEG, 0)
    for g in range(GRP):
        for part in range(3):
            k[part * GRP + g, K_SEL + g * P:K_SEL + (g + 1) * P] = 1
    return k


class Chain:

    def __init__(self, eng, sem):
        self.eng, self.sem, self.count, self.turns = eng, sem, 0, 0

    def mark(self, ins):
        ins.then_inc(self.sem, 1)
        self.count += 1
        return self.count + self.turns

    def wait(self, value=None):
        self.eng.wait_ge(self.sem, self.count + self.turns if value is None else value)

    def begin(self, turn, per_turn):
        self.start, self.per_turn = self.count, per_turn
        self.turns = turn * per_turn

    def end(self, turns):
        assert self.count - self.start == self.per_turn, (self.count - self.start, self.per_turn)
        self.count = self.start + turns * self.per_turn
        self.turns = 0


def build_block(nc, x, w_g, b_g, w_gu, w_d, b_gu, b_d, b_attn, b_proj, w_attn, w_proj, konst, out):
    ctx = ExitStack()
    with ctx:
        def sb(name, shape, dt=F32):
            return ctx.enter_context(nc.sbuf_tensor(name, shape, dt))

        def sem(name):
            return ctx.enter_context(nc.semaphore(name))

        banks = ctx.enter_context(nc.psum_tensor("banks", [P, 8, 512], F32))
        bank = [banks[:, i, :] for i in range(8)]

        rows_dram = nc.dram_tensor("rows_by_expert", (E * REGION, C), F32, kind="Internal").ap()
        stack_dram = [[nc.dram_tensor(f"{n}_by_part{i}", (P, PARTS, QUAD * P), BF16, kind="Internal").ap() for i in range(2)] for n in "qk"]
        results_dram = nc.dram_tensor("results_by_tile", (TILES * P, C), F32, kind="Internal").ap()

        xs = sb("x_resident", [P, QT + NT, C])
        xr = xs[:, QT:, :]
        kc = sb("konst_sb", [P, K_W])
        ident = kc[:, K_ID:K_ID + P]
        tri = sb("tri", [P, P], BF16)
        ones = sb("ones", [P, P], BF16)
        utri = sb("utri", [E, 2 * E], BF16)
        wg = sb("wg", [P, E])
        bg = sb("bg", [P, E])
        w_all = sb("w_experts", [P, E * EW])
        zeros = sb("zeros", [P, C])
        NB = E + 1
        bias_in = sb("bias_in", [NB, EW])
        bias_hi = sb("bias_hi", [NB, EW], BF16)
        bias_mid = sb("bias_mid", [NB, EW], BF16)
        bias_lo = sb("bias_lo", [NB, EW], BF16)
        bias3 = sb("bias3", [3, NB * EW], BF16)

        vz = sb("values_spread", [P, SLOTS * QT * GRP, GRP * ROWS_V])
        xn = vz.rearrange("p a w -> p (a w)")[:, 0:NT * C].rearrange("p (n c) -> p n c", n=NT)
        st6 = sb("st6", [P, NT, 6])
        mv = sb("mv", [P, NT, 2])
        veps = sb("veps", [P, NT])
        rstd = sb("rstd", [P, NT])
        neghalf = sb("neghalf", [P, QUAD])
        xnT = sb("xnT", [P, 2, QUAD * P])
        lg = sb("lg", [P, NQ, QUAD, E])
        mx = sb("mx", [P, NT, 8])
        mi = sb("mi", [P, NT, 8], U32)
        mif = sb("mif", [P, NT, TOPK])
        oh = sb("oh", [P, NT, TOPK, E], BF16)
        mask = sb("mask", [P, NT, E], BF16)
        macc = sb("macc", [P, NQ + 1, E], BF16)
        msum = sb("msum", [P, NQ, E])
        gap = sb("gap", [P, NT])
        rank = sb("rank", [P, NQ, QUAD, E])
        rsel = sb("rsel", [P, NQ, QUAD * TOPK, E])
        posf = sb("posf", [P, NT * TOPK])
        posi = sb("posi", [P, NT * TOPK], I32)
        wts = sb("wts", [P, TOPK, NT])
        cnt = sb("cnt", [E, P])
        cntr = sb("cntr", [E, P])
        ntile = sb("ntile", [E, P], BF16)
        cum = sb("cum", [P, 2 * E])
        delta = sb("delta", [P, E])
        below = sb("below", [P, 2 * E])
        hot = sb("hot", [P, E])
        rowof = sb("rowof", [P, E])
        tmp2 = sb("tmp2", [P, 2, E])
        tabf = sb("tabf", [P, 2])
        tabc = sb("tabc", [P, 2], I32)
        zrow = sb("zrow", [E, 1], I32)
        tab = sb("tab", [1, 2 * TILES + E], I32)
        dsel = rsel.rearrange("p q k e -> p (q k) e")
        dsum = sb("dsum", [P, NT * TOPK])
        resi = sb("resi", [P, NT * TOPK], I32)
        xt = sb("xt", [P, UNROLL, C])
        xT = sb("xT", [P, 2, 2 * P])
        sig = sb("sig", [P, 2, 2, F])
        upc = sb("upc", [P, 2, 2, F])
        gT = sb("gT", [P, 2, 2 * P])
        ysb = sb("ysb", [P, 2, 2, C])
        w_in = sb("w_attn_sb", [P, 3 * C])
        w_out = sb("w_proj_sb", [P, C])
        bqk = sb("bqk", [P, 2])
        identb = sb("identb", [P, P], BF16)
        mask_q = sb("mask_q", [P, P], BF16)
        mask_k = sb("mask_k", [P, P], BF16)
        select = sb("select", [3 * GRP, GRP, P], BF16)
        a_st6 = sb("a_st6", [P, QUAD, 6])
        a_mv = sb("a_mv", [P, QUAD, 2])
        a_ve = sb("a_ve", [P, QUAD])
        a_rs = sb("a_rs", [P, QUAD])
        xa = xnT[:, 0, :].rearrange("p (n c) -> p n c", n=QUAD)
        xaT = xnT[:, 1, :]
        parts = [sb(f"{n}_parts", [P, 3, QUAD * P], BF16) for n in "qk"]
        rest = [buf.rearrange("p a n f -> p (a n f)") for buf in (sig, upc)]
        stack = [sb(f"{n}_stack", [P, SLOTS // 2, H // 2, QUAD * P], BF16) for n in "qk"]
        mraw = sb("mraw", [P, QT, GRP])
        mrest = sb("mrest", [P, QT, GRP])
        mparts = sb("mparts", [P, QT, 3, GRP], BF16)
        mT = sb("mT", [3 * GRP, 2, QT * P], BF16)
        pT = sb("pT", [P, 2, 3 * GRP * P])
        ysum = sb("ysum", [P, QT * 2 * P])
        rsum = sb("rsum", [P, QT * 2 * P])
        yT = sb("yT", [P, QT * P])
        a_resi = sb("a_resi", [P, QUAD * TOPK], I32)
        spare = sb("spare", [P, 1])
        yg = sb("yg", [P, 2, QUAD * TOPK, C])
        a_yg = yg[:, 0, :, :]
        resg = sb("resg", [P, 2, QUAD * TOPK], I32)

        s_const = sem("s_const")
        s_wexp = sem("s_wexp")
        s_x = [sem(f"s_x{i}") for i in range(NQ)]
        s_bias3 = sem("s_bias3")
        s_setup = sem("s_setup")
        s_vec = sem("s_vec")
        s_act = sem("s_act")
        s_pool = sem("s_pool")
        s_veps = sem("s_veps")
        s_rstd = sem("s_rstd")
        s_xn = sem("s_xn")
        s_xnTp = sem("s_xnTp")
        s_xnT = sem("s_xnT")
        s_logit = sem("s_logit")
        s_mask = sem("s_mask")
        s_rank = sem("s_rank")
        s_pos = sem("s_pos")
        s_scat = sem("s_scat")
        s_count = sem("s_count")
        s_ntile = sem("s_ntile")
        s_cum = sem("s_cum")
        s_table = sem("s_table")
        s_tab = sem("s_tab")
        s_zero = sem("s_zero")
        s_resi = sem("s_resi")
        s_wts = sem("s_wts")
        s_xt = [sem(f"s_xt{i}") for i in range(UNROLL)]
        s_xTp = sem("s_xTp")
        s_xT = sem("s_xT")
        s_gu = sem("s_gu")
        s_sig = sem("s_sig")
        s_gated = sem("s_gated")
        s_gTp = sem("s_gTp")
        s_gT = sem("s_gT")
        s_y = sem("s_y")
        s_ysb = sem("s_ysb")
        s_store = [sem(f"s_store{i}") for i in range(2)]
        s_resg = [sem(f"s_resg{i}") for i in range(2)]
        s_got = [sem(f"s_got{i}") for i in range(2)]
        s_comb = sem("s_comb")
        s_out = sem("s_out")
        s_watt = sem("s_watt")
        s_asetup = sem("s_asetup")
        a_resg = sem("a_resg")
        a_mid = sem("a_mid")
        a_got = sem("a_got")
        a_veps = sem("a_veps")
        a_rstd = sem("a_rstd")
        a_xn = sem("a_xn")
        a_Tp = sem("a_Tp")
        a_xT = sem("a_xT")
        a_made = [sem(f"a_{n}_made") for n in "qk"]
        a_high = [sem(f"a_{n}_high") for n in "qk"]
        a_rest = [sem(f"a_{n}_rest") for n in "qk"]
        a_low = [sem(f"a_{n}_low") for n in "qk"]
        a_spread = [sem(f"a_{n}_spread") for n in "qk"]
        a_v = sem("a_v")
        a_vs = sem("a_vs")
        a_s = sem("a_s")
        a_max = sem("a_max")
        a_mTp = sem("a_mTp")
        a_mT = sem("a_mT")
        a_st = sem("a_st")
        a_exp = sem("a_exp")
        a_pv = sem("a_pv")
        a_ysum = sem("a_ysum")
        a_y = sem("a_y")
        s_vz = sem("s_vz")
        a_proj = sem("a_proj")
        a_x2 = sem("a_x2")
        a_stack = [sem(f"a_stack{i}") for i in range(2)]

        x_t = x.rearrange("(n p) c -> p n c", p=P)
        out_t = out.rearrange("(n p) c -> p n c", p=P)
        PAIRS = TILES // 2

        block = ctx.enter_context(nc.Block())

        def stack_all(sp):
            def stack_pair(turn, half):
                x = turn * 2 + half
                first = isinstance(x, int)
                scored = None if first else sp.snap(x * 8 - 8)
                for which in range(2):
                    sp.wait_ge(a_low[which], x + 1)
                    if which == 0 and not first:
                        sp.wait_ge(a_st, scored)
                    src, dst = parts[which], stack_dram[which][half]
                    if which == 0:
                        for a in range(2):
                            sp.dma_start(dst[:, 3 * a:3 * a + 3, :], src[:, a:a + 1, :].to_broadcast([P, 3, QUAD * P])).then_inc(a_spread[0], 16)
                        sp.dma_start(dst[:, 6:8, :], src[:, 2:3, :].to_broadcast([P, 2, QUAD * P])).then_inc(a_spread[0], 16)
                    else:
                        for a in range(2):
                            sp.dma_start(dst[:, 3 * a:3 * a + 3, :], src[:, :, :]).then_inc(a_spread[1], 16)
                        sp.dma_start(dst[:, 6:8, :], src[:, 0:2, :]).then_inc(a_spread[1], 16)
                for which in range(2):
                    sp.wait_ge(a_spread[which], x * 48 + 48)
                    sp.dma_start(stack[which][:, half, :, :], stack_dram[which][half].rearrange("(m r) p t -> (r p) m t", m=H // 2)).then_inc(a_stack[half], 16)

            for half in range(2):
                stack_pair(0, half)
            with sp.Fori(1, TURNS_A) as t:
                for half in range(2):
                    stack_pair(t, half)

        @block.sync
        def _(sp):
            sp.dma_start(kc[:, :], konst).then_inc(s_const, 16)
            sp.dma_start(xr[:, 0:QUAD, :], x_t[:, 0:QUAD, :]).then_inc(s_x[0], 16)
            sp.dma_start(wg[:, :], w_g).then_inc(s_const, 16)
            sp.dma_start(bg[:, :], b_g.partition_broadcast(P)).then_inc(s_const, 16)
            for q in range(1, NQ):
                sp.dma_start(xr[:, QUAD * q:QUAD * q + QUAD, :], x_t[:, QUAD * q:QUAD * q + QUAD, :]).then_inc(s_x[q], 16)
            sp.dma_start(bias_in[0:E, 0:2 * F], b_gu).then_inc(s_bias3, 16)
            sp.dma_start(bias_in[0:E, 2 * F:EW], b_d).then_inc(s_bias3, 16)
            sp.dma_start(bias_in[E:NB, 0:C], b_attn[2:3, :]).then_inc(s_bias3, 16)
            sp.dma_start(bias_in[E:NB, C:2 * C], b_proj).then_inc(s_bias3, 16)
            sp.dma_start(bias_in[E:NB, 2 * C:EW], b_proj).then_inc(s_bias3, 16)
            w_of_expert = w_all.rearrange("p (e w) -> p e w", e=E)
            sp.dma_start(w_of_expert[:, :, 0:2 * F], w_gu.rearrange("p (e w) -> p e w", e=E)).then_inc(s_wexp, 16)
            sp.dma_start(w_of_expert[:, :, 2 * F:EW], w_d.rearrange("p (e w) -> p e w", e=E)).then_inc(s_wexp, 16)
            sp.wait_ge(s_setup, 2)
            for r, part in enumerate((bias_hi, bias_mid, bias_lo)):
                sp.dma_start(bias3[r:r + 1, :].rearrange("a (e w) -> a e w", e=NB), part[:, :]).then_inc(s_bias3, 16)

            sp.dma_start(w_in[:, :], w_attn).then_inc(s_watt, 16)
            sp.dma_start(w_out[:, :], w_proj).then_inc(s_watt, 16)
            for i in range(2):
                sp.dma_start(bqk[:, i:i + 1], b_attn[i:i + 1, :].rearrange("a c -> c a")).then_inc(s_watt, 16)

            for f in range(2):
                if f == 1:
                    stack_all(sp)
                sp.wait_ge(s_table, 1 + f)
                for k in range(2):
                    sp.dma_start(tab[0:1, k * TILES:(k + 1) * TILES], tabc[0:TILES, k:k + 1]).then_inc(s_tab, 16)
                sp.dma_start(tab[0:1, 2 * TILES:2 * TILES + E], zrow[:, :]).then_inc(s_tab, 16)
                sp.wait_ge(s_tab, 48 * (f + 1))
                with sp.Fori(0, E // 4) as e:
                    for r in registers(nc, sp, tab[0:1, bass.ds(e * 4 + 2 * TILES, 4)], E * REGION - P):
                        sp.dma_start(rows_dram[bass.ds(r, P), :], zeros[:, :]).then_inc(s_zero, 16)
                sp.wait_ge(s_zero, 16 * E * (f + 1))
                sp.wait_ge(s_scat, 16 * NT * TOPK * (f + 1))

                def rows_of_tiles(turn, u):
                    return registers(nc, sp, tab[0:1, bass.ds(turn * UNROLL + (TILES + u), 4)], E * REGION - P)

                def load_tile(r, u):
                    sp.dma_start(xt[:, u, :], rows_dram[bass.ds(r, P), :]).then_inc(s_xt[u], 16)

                for u in range(0, UNROLL, 4):
                    for i, r in enumerate(rows_of_tiles(0, u)):
                        load_tile(r, u + i)
                with sp.Fori(1, TURNS) as t:
                    for k in range(DUOS):
                        sp.wait_ge(s_xTp, t * DUOS + (k + 1 - DUOS) + f * PAIRS)
                        if k % 2 == 0:
                            rows = rows_of_tiles(t, 2 * k)
                        for i in range(2):
                            load_tile(rows[k % 2 * 2 + i], 2 * k + i)
            for q in range(NQ):
                sp.wait_ge(s_comb, q + 1)
                sp.dma_start(out_t[:, QUAD * q:QUAD * q + QUAD, :], xr[:, QUAD * q:QUAD * q + QUAD, :]).then_inc(s_out, 16)
            sp.wait_ge(s_out, 16 * NQ)

        @block.gpsimd
        def _(pool):
            nc.gpsimd.memset(zeros[:, :], 0.0).then_inc(s_pool, 1)
            nc.gpsimd.memset(neghalf[:, :], -0.5).then_inc(s_pool, 1)
            pool.wait_ge(s_pool, 2)
            for f in range(2):
                if f == 1:
                    with pool.Fori(1, B // 2 + 1) as x:
                        pool.wait_ge(s_pool, 2)
                        pool.wait_ge(a_resg, x)
                        for c in range(QUAD * TOPK):
                            pool.indirect_dma_start(
                                out=a_yg[:, c, :], out_offset=None, in_=results_dram,
                                in_offset=bass.IndirectOffsetOnAxis(ap=a_resi[:, c:c + 1], axis=0)).then_inc(a_got, 16)
                        pool.wait_ge(a_veps, x)
                        nc.gpsimd.tensor_tensor(a_rs[:, :], a_ve[:, :], neghalf[:, :], ALU.pow).then_inc(a_rstd, 1)
                        for which in range(2):
                            pool.wait_ge(s_pool, 2)
                            pool.wait_ge(a_rest[which], x)
                            nc.gpsimd.tensor_copy(parts[which][:, 1, :], rest[which][:, :]).then_inc(a_mid, 1)
                            pool.wait_ge(a_mid, x * 2 + (which - 1))
                            nc.gpsimd.tensor_tensor(parts[which][:, 2, :], rest[which][:, :], parts[which][:, 1, :],
                                                    ALU.subtract).then_inc(a_low[which], 1)

                def root(q):
                    pool.wait_ge(s_veps, f * NQ + q + 1)
                    nc.gpsimd.tensor_tensor(rstd[:, QUAD * q:QUAD * q + QUAD], veps[:, QUAD * q:QUAD * q + QUAD],
                                            neghalf[:, :], ALU.pow).then_inc(s_rstd, 1)

                def scatter(q):
                    pool.wait_ge(s_pos, f * NQ + q + 1)
                    for i in range(QUAD):
                        t = QUAD * q + i
                        for k in range(TOPK):
                            c = t * TOPK + k
                            pool.indirect_dma_start(
                                out=rows_dram, out_offset=bass.IndirectOffsetOnAxis(ap=posi[:, c:c + 1], axis=0),
                                in_=xn[:, t, :], in_offset=None).then_inc(s_scat, 16)

                for q in range(NQ + 3):
                    if q < NQ:
                        root(q)
                    if q >= 3:
                        scatter(q - 3)

                if f == 0:
                    pool.wait_ge(s_scat, 16 * NT * TOPK)
                    nc.gpsimd.memset(vz[:, :, :], 0.0).then_inc(s_pool, 1)
                    pool.wait_ge(s_pool, 3)
                    nc.gpsimd.memset(vz[:, :, :].rearrange("p a (j w) -> p a j w", j=GRP)[:, :, :, P // 4:P // 4 + D], 1.0).then_inc(s_vz, 1)
                with pool.Fori(0, TURNS) as t:
                    for k in range(DUOS):
                        pool.wait_ge(s_ysb, t * DUOS + (k + 1 + f * PAIRS))
                        pool.dma_start(results_dram[bass.ds((t * DUOS + k) * (2 * P), 2 * P), :].rearrange("(n p) c -> p n c", p=P),
                                       ysb[:, k % 2, :, :]).then_inc(s_store[k % 2], 16)

                for k in range(2):
                    pool.wait_ge(s_store[k], 16 * (PAIRS // 2) * (f + 1))
            with pool.Fori(1, NQ // 2 + 1) as h:
                for u in range(2):
                    pool.wait_ge(s_pool, 2)
                    pool.wait_ge(s_resg[u], h)
                    for c in range(QUAD * TOPK):
                        pool.indirect_dma_start(
                            out=yg[:, u, c, :], out_offset=None, in_=results_dram,
                            in_offset=bass.IndirectOffsetOnAxis(ap=resg[:, u, c:c + 1], axis=0)).then_inc(s_got[u], 16)

        def attention_scalar(act):
            def evac_xT(x):
                act.wait_ge(a_Tp, x + 1)
                nc.scalar.activation(xaT[:, :], bank[7][:, :], ACT.Identity).then_inc(a_xT, 1)

            def high(which, x):
                act.wait_ge(a_made[which], x + 1)
                beyond_first(act, a_spread[which], x * 48)
                nc.scalar.activation(parts[which][:, 0, :], bank[7][:, :], ACT.Identity, bias=bqk[:, which:which + 1]).then_inc(a_high[which], 1)

            def evac_v(x, half):
                act.wait_ge(a_v, x + 1)
                to = vz[:, half * 2 * QT * GRP:(half + 1) * 2 * QT * GRP, :].rearrange("p a (j w) -> p a j w", j=GRP)
                nc.scalar.activation(to[:, :, :, 0:D], bank[7][:, :].rearrange("p (a j d) -> p a j d", j=GRP, d=D), ACT.Identity).then_inc(a_vs, 1)

            def evac_max(t, s):
                n = t * UNITS + s
                act.wait_ge(a_mTp, n + 1)
                beyond_first(act, a_st, n - 1)
                nc.scalar.activation(mT[:, s % 2, :], bank[7][0:3 * GRP, 0:QT * P], ACT.Identity, scale=-1.0).then_inc(a_mT, 1)

            def exp(t, s):
                n = t * UNITS + s
                act.wait_ge(a_st, n + 1)
                nc.scalar.activation(pT[:, s % 2, :],
                                     banks[:, 3:6, :].rearrange("p a q -> p (a q)"), ACT.Exp, scale=SCALE).then_inc(a_exp, 1)

            def evac_sums(b):
                act.wait_ge(a_pv, (b + 1) * GRP)
                act.wait_ge(a_y, b + 1)
                nc.scalar.activation(ysum[:, :], bank[6][:, :], ACT.Identity).then_inc(a_ysum, 1)

            act.wait_ge(s_vz, 1)
            evac_xT(0)
            high(0, 0)
            high(1, 0)
            evac_v(0, 0)
            evac_xT(1)
            evac_max(0, 0)

            def unit(t, s):
                t, s = t + s // UNITS, s % UNITS
                steps = Steps(t, s)
                if steps.max_next:
                    evac_max(*after(t, s, 1))
                exp(t, s)
                if steps.q is not None:
                    high(0, steps.q)
                if steps.k is not None:
                    high(1, steps.k)
                if steps.v is not None:
                    evac_v(steps.v, steps.half)
                if steps.x is not None:
                    evac_xT(steps.x)
                if steps.sums is not None:
                    evac_sums(steps.sums)

            attention_loop(act, unit, None)
            evac_sums(B - 1)

        @block.scalar
        def _(act):
            for f in range(2):
                if f == 1:
                    attention_scalar(act)
                for q in range(NQ):
                    act.wait_ge(s_xnTp, f * NQ + q + 1)
                    if q >= 2:
                        act.wait_ge(s_logit, f * NQ + q - 1)
                    nc.scalar.activation(xnT[:, q % 2, :], bank[q % 2][:, :], ACT.Identity).then_inc(s_xnT, 1)
                act.wait_ge(s_mask, (f + 1) * NQ)
                nc.scalar.activation(wts[:, 0, :], gap[:, :], ACT.Sigmoid).then_inc(s_wts, 1)
                nc.scalar.activation(wts[:, 1, :], gap[:, :], ACT.Sigmoid, scale=-1.0).then_inc(s_wts, 1)

                def evac_x(t, k):
                    n = t * DUOS + k + f * PAIRS
                    act.wait_ge(s_xTp, n + 1)
                    nc.scalar.activation(xT[:, k % 2, :], bank[k % 2][:, 0:2 * P], ACT.Identity).then_inc(s_xT, 1)

                def sigmoid(t, k):
                    n = t * DUOS + k + f * PAIRS
                    act.wait_ge(s_gu, n + 1)
                    nc.scalar.activation(sig[:, k % 2, :, :], bank[2 + k % 2][:, :].rearrange("p (n w) -> p n w", n=2)[:, :, 0:F],
                                         ACT.Sigmoid, scale=ALPHA).then_inc(s_sig, 1)

                def evac_g(t, k):
                    n = t * DUOS + k + f * PAIRS
                    act.wait_ge(s_gTp, n + 1)
                    nc.scalar.activation(gT[:, k % 2, :], bank[4 + k % 2][:, 0:2 * P], ACT.Identity).then_inc(s_gT, 1)

                def evac_y(t, k):
                    n = t * DUOS + k + f * PAIRS
                    act.wait_ge(s_y, n + 1)
                    beyond_first(act, s_store[k % 2], (t * (DUOS // 2) + (k // 2 + f * PAIRS // 2)) * 16)
                    nc.scalar.activation(ysb[:, k % 2, :, :].rearrange("p n c -> p (n c)"), bank[6 + k % 2][:, 0:2 * P],
                                         ACT.Identity).then_inc(s_ysb, 1)

                expert_pipeline(act, evac_x, sigmoid, evac_g, evac_y)

        def attention_vector(dve, ch):
            def name_rows(x):
                nc.vector.tensor_copy(a_resi[:, :], resi[:, bass.ds(x * (QUAD * TOPK), QUAD * TOPK)]).then_inc(a_resg, 1)

            def row(x, i):
                return xr[:, bass.ds(x * QUAD + i, 1), :].rearrange("p a c -> p (a c)")

            def combine(x):
                dve.wait_ge(a_got, (x + 1) * (16 * QUAD * TOPK))
                for k in range(TOPK):
                    for i in range(QUAD):
                        ch.mark(nc.vector.scalar_tensor_tensor(out=row(x, i), in0=a_yg[:, TOPK * i + k, :], scalar=wts[:, k, bass.ds(x * QUAD + i, 1)],
                                                               in1=row(x, i), op0=ALU.mult, op1=ALU.add))
                    if k < TOPK - 1:
                        ch.wait()

            def settle():
                ch.wait()
                ch.mark(nc.vector.memset(spare[:, :], 0.0))

            def stats(x):
                settle()
                for i in range(QUAD):
                    ch.mark(nc.vector.bn_stats(a_st6[:, i, :], row(x, i)))
                settle()
                for i in range(QUAD):
                    ch.mark(nc.vector.bn_aggr(a_mv[:, i, :], a_st6[:, i, :]))
                ch.wait()
                nc.vector.tensor_scalar(a_ve[:, :], a_mv[:, :, 1], EPS, None, ALU.add).then_inc(a_veps, 1)

            def normalise(x):
                dve.wait_ge(a_rstd, x + 1)
                beyond_first(dve, a_Tp, x)
                for i in range(QUAD):
                    last = nc.vector.tensor_scalar(xa[:, i, :], row(x, i), a_mv[:, i, 0:1], a_rs[:, i:i + 1], ALU.subtract, ALU.mult)
                last.then_inc(a_xn, 1)

            def split_rest(which, x):
                dve.wait_ge(a_high[which], x + 1)
                beyond_first(dve, a_low[which], x)
                nc.vector.scalar_tensor_tensor(out=rest[which][:, :], in0=bank[7][:, :], scalar=bqk[:, which:which + 1],
                                               in1=parts[which][:, 0, :], op0=ALU.add, op1=ALU.subtract).then_inc(a_rest[which], 1)

            def row_max(t, s):
                n = t * UNITS + s
                dve.wait_ge(a_s, n + 1)
                beyond_first(dve, a_mTp, n)
                ch.mark(nc.vector.tensor_reduce(mraw[:, 0, :], bank[0][:, :].rearrange("p (g k) -> p g k", g=GRP), AX.X, ALU.max))
                ch.mark(nc.vector.tensor_reduce(mraw[:, 1, :], banks[:, 1:3, :].rearrange("p a (g k) -> p (a g) k", g=2), AX.X, ALU.max))
                ch.wait()
                ch.mark(nc.vector.tensor_copy(mparts[:, :, 0, :], mraw[:, :, :]))
                ch.wait()
                ch.mark(nc.vector.tensor_tensor(mrest[:, :, :], mraw[:, :, :], mparts[:, :, 0, :], ALU.subtract))
                ch.wait()
                ch.mark(nc.vector.tensor_copy(mparts[:, :, 1, :], mrest[:, :, :]))
                ch.wait()
                nc.vector.tensor_tensor(mparts[:, :, 2, :], mrest[:, :, :], mparts[:, :, 1, :], ALU.subtract).then_inc(a_max, 1)

            def divide(b):
                dve.wait_ge(a_ysum, b + 2)
                ch.mark(nc.vector.reciprocal(rsum[:, :], ysum[:, :]))
                ch.wait()
                for g in range(GRP):
                    r, c = g % 2 * HALF, slice(g // 2 * T, (g // 2 + 1) * T)
                    last = nc.vector.tensor_tensor(yT[g * 32:(g + 1) * 32, :], ysum[r:r + 32, c], rsum[r + 32:r + 64, c], ALU.mult)
                last.then_inc(a_y, 1)

            def add_attention(b):
                dve.wait_ge(a_proj, b + 2)
                rows = xs[:, bass.ds((b + 1) * QT, QT), :].rearrange("p n c -> p (n c)")
                nc.vector.tensor_tensor(rows, bank[7][:, 0:QT * C], rows, ALU.add).then_inc(a_x2, 1)

            name_rows(0)
            for x in range(2):
                combine(x)
                if x == 0:
                    name_rows(1)
                stats(x)
                normalise(x)
                if x == 0:
                    split_rest(0, 0)
                    split_rest(1, 0)
            row_max(0, 0)
            row_max(0, 1)

            def unit(t, s):
                t, s = t + s // UNITS, s % UNITS
                steps = Steps(t, s)
                if steps.scores_next:
                    row_max(*after(t, s, 2))
                if steps.q is not None:
                    split_rest(0, steps.q)
                if steps.k is not None:
                    split_rest(1, steps.k)
                if steps.divide is not None:
                    divide(steps.divide)
                if steps.add is not None:
                    add_attention(steps.add)
                if steps.name is not None:
                    name_rows(steps.name)
                if steps.combine is not None:
                    combine(steps.combine)
                    stats(steps.combine)
                if steps.normalise is not None:
                    normalise(steps.normalise)

            attention_loop(dve, unit, (ch, ATT_CHAIN))
            divide(B - 1)
            add_attention(B - 1)

        @block.vector
        def _(dve):
            ch = Chain(dve, s_vec)
            dve.wait_ge(s_const, 48)
            nc.vector.tensor_copy(tri[:, :], kc[:, K_TRI:K_TRI + P]).then_inc(s_setup, 1)
            ch.mark(nc.vector.memset(ones[:, :], 1.0))
            ch.mark(nc.vector.tensor_copy(utri[:, :], kc[0:E, K_U:K_U + 2 * E]))
            ch.mark(nc.vector.memset(macc[:, :, :], 0.0))

            nc.vector.tensor_copy(identb[:, :], ident).then_inc(s_asetup, 1)
            nc.vector.tensor_copy(mask_q[:, :], kc[:, K_MQ:K_MQ + P]).then_inc(s_asetup, 1)
            nc.vector.tensor_copy(mask_k[:, :], kc[:, K_MK:K_MK + P]).then_inc(s_asetup, 1)
            nc.vector.memset(ysum[:, :], 1.0).then_inc(a_ysum, 1)
            nc.vector.memset(xs[:, 0:QT, :], 0.0).then_inc(s_asetup, 1)
            nc.vector.tensor_copy(select[:, :, :].rearrange("p a k -> p (a k)"), kc[0:3 * GRP, K_SEL:K_SEL + GRP * P]).then_inc(s_asetup, 1)

            for f in range(2):
                if f == 1:
                    attention_vector(dve, ch)

                def stats(q):
                    if f == 0:
                        dve.wait_ge(s_x[q], 16)
                    for t in range(QUAD * q, QUAD * q + QUAD):
                        ch.mark(nc.vector.bn_stats(st6[:, t, :], xr[:, t, :]))
                    ch.wait()
                    for t in range(QUAD * q, QUAD * q + QUAD):
                        ch.mark(nc.vector.bn_aggr(mv[:, t, :], st6[:, t, :]))
                    ch.wait()
                    nc.vector.tensor_scalar(veps[:, QUAD * q:QUAD * q + QUAD], mv[:, QUAD * q:QUAD * q + QUAD, 1],
                                            EPS, None, ALU.add).then_inc(s_veps, 1)

                def normalise(q):
                    dve.wait_ge(s_rstd, f * NQ + q + 1)
                    for t in range(QUAD * q, QUAD * q + QUAD):
                        last = nc.vector.tensor_scalar(xn[:, t, :], xr[:, t, :], mv[:, t, 0:1], rstd[:, t:t + 1],
                                                       ALU.subtract, ALU.mult)
                    last.then_inc(s_xn, 1)

                def top2(q):
                    ts = slice(QUAD * q, QUAD * q + QUAD)
                    dve.wait_ge(s_logit, f * NQ + q + 1)
                    ch.mark(nc.vector.tensor_tensor(lg[:, q, :, :], bank[2 + q % 2][:, 0:QUAD * E].rearrange("p (n e) -> p n e", n=QUAD),
                                                    bg[:, :].unsqueeze(1).to_broadcast([P, QUAD, E]), ALU.add))
                    ch.wait()
                    for i in range(QUAD):
                        ch.mark(nc.vector.max(mx[:, QUAD * q + i, :], lg[:, q, i, :]))
                    ch.wait()
                    for i in range(QUAD):
                        ch.mark(nc.vector.max_index(mi[:, QUAD * q + i, :], mx[:, QUAD * q + i, :], lg[:, q, i, :]))
                    ch.mark(nc.vector.tensor_tensor(gap[:, ts], mx[:, ts, 0], mx[:, ts, 1], ALU.subtract))
                    ch.wait()
                    ch.mark(nc.vector.tensor_copy(mif[:, ts, :], mi[:, ts, 0:TOPK]))
                    ch.wait()
                    ch.mark(nc.vector.tensor_tensor(
                        oh[:, ts, :, :].rearrange("p n k e -> p (n k) e"),
                        kc[:, K_E:K_E + E].unsqueeze(1).to_broadcast([P, QUAD * TOPK, E]),
                        mif[:, ts, :].rearrange("p n k -> p (n k)").unsqueeze(2).to_broadcast([P, QUAD * TOPK, E]), ALU.is_equal))
                    ch.wait()
                    ch.mark(nc.vector.tensor_tensor(mask[:, ts, :], oh[:, ts, 0, :], oh[:, ts, 1, :], ALU.add))
                    ch.wait()
                    ch.mark(nc.vector.tensor_reduce(msum[:, q, :], mask[:, ts, :].rearrange("p n e -> p e n"), AX.X, ALU.add))
                    ch.wait()
                    nc.vector.tensor_tensor(macc[:, q + 1, :], macc[:, q, :], msum[:, q, :], ALU.add).then_inc(s_mask, 1)

                def positions(q):
                    dve.wait_ge(s_rank, f * NQ + q + 1)
                    ch.mark(nc.vector.tensor_tensor(rank[:, q, :, :], bank[4 + q % 2][:, 0:QUAD * E].rearrange("p (n e) -> p n e", n=QUAD),
                                                    kc[:, K_BASE:K_BASE + E].unsqueeze(1).to_broadcast([P, QUAD, E]), ALU.add))
                    ch.wait()
                    for k in range(TOPK):
                        ch.mark(nc.vector.tensor_tensor(
                            rsel[:, q, :, :].rearrange("p (n k) e -> p n k e", k=TOPK)[:, :, k, :],
                            oh[:, QUAD * q:QUAD * q + QUAD, k, :], rank[:, q, :, :], ALU.mult))
                    ch.wait()
                    cs = slice(QUAD * TOPK * q, QUAD * TOPK * (q + 1))
                    ch.mark(nc.vector.tensor_reduce(posf[:, cs], rsel[:, q, :, :], AX.X, ALU.add))
                    ch.wait()
                    nc.vector.tensor_copy(posi[:, cs], posf[:, cs]).then_inc(s_pos, 1)

                def split_biases():
                    dve.wait_ge(s_bias3, 80)
                    ch.mark(nc.vector.tensor_copy(bias_hi[:, :], bias_in[:, :]))
                    ch.wait()
                    ch.mark(nc.vector.tensor_tensor(bias_in[:, :], bias_in[:, :], bias_hi[:, :], ALU.subtract))
                    ch.wait()
                    ch.mark(nc.vector.tensor_copy(bias_mid[:, :], bias_in[:, :]))
                    ch.wait()
                    ch.mark(nc.vector.tensor_tensor(bias_in[:, :], bias_in[:, :], bias_mid[:, :], ALU.subtract))
                    ch.wait()
                    nc.vector.tensor_copy(bias_lo[:, :], bias_in[:, :]).then_inc(s_setup, 1)

                for q in range(NQ + 2):
                    if 1 <= q <= NQ:
                        top2(q - 1)
                    if q < NQ:
                        stats(q)
                    if 2 <= q:
                        positions(q - 2)
                    if q < NQ:
                        normalise(q)
                    if f == 0 and q == 2:
                        split_biases()
                dve.wait_ge(s_count, f + 1)
                ch.mark(nc.vector.tensor_scalar(cnt[:, :], bank[6][0:E, 0:P], 1.0 / P, (P - 1.0) / P - 0.5 + 0.5 / P, ALU.mult, ALU.add))
                ch.wait()
                ch.mark(nc.vector.tensor_scalar(cntr[:, :], cnt[:, :], ROUND, None, ALU.add))
                ch.wait()
                nc.vector.tensor_scalar(ntile[:, :], cntr[:, :], -ROUND, None, ALU.add).then_inc(s_ntile, 1)
                ch.mark(nc.vector.tensor_scalar(zrow[:, :], bank[6][0:E, 0:1], kc[0:E, K_BASEP:K_BASEP + 1], None, ALU.add))
                dve.wait_ge(s_cum, f + 1)
                ch.mark(nc.vector.tensor_copy(cum[:, :], bank[7][:, 0:2 * E]))
                ch.wait()
                ch.mark(nc.vector.scalar_tensor_tensor(out=delta[:, :], in0=cum[:, E:2 * E], scalar=float(P),
                                                       in1=kc[:, K_BASE:K_BASE + E], op0=ALU.mult, op1=ALU.subtract))
                ch.mark(nc.vector.tensor_scalar(below[:, :], cum[:, :], kc[:, K_ROW:K_ROW + 1], None, ALU.is_le))
                ch.wait()
                ch.mark(nc.vector.tensor_tensor(hot[:, :], below[:, E:2 * E], below[:, 0:E], ALU.subtract))
                ch.mark(nc.vector.tensor_scalar(rowof[:, :], delta[:, :], -1.0, kc[:, K_ROW128:K_ROW128 + 1], ALU.mult, ALU.add))
                ch.wait()
                ch.mark(nc.vector.tensor_tensor(tmp2[:, 0, :], hot[:, :], kc[:, K_EW:K_EW + E], ALU.mult))
                ch.mark(nc.vector.tensor_tensor(tmp2[:, 1, :], hot[:, :], rowof[:, :], ALU.mult))
                ch.wait()
                ch.mark(nc.vector.tensor_reduce(tabf[:, :], tmp2[:, :, :], AX.X, ALU.add))
                ch.wait()
                nc.vector.tensor_copy(tabc[:, :], tabf[:, :]).then_inc(s_table, 1)
                ch.mark(nc.vector.tensor_tensor(dsel[:, :, :], oh[:, :, :, :].rearrange("p n k e -> p (n k) e"),
                                                delta[:, :].unsqueeze(1).to_broadcast([P, NT * TOPK, E]), ALU.mult))
                ch.wait()
                ch.mark(nc.vector.tensor_reduce(dsum[:, :], dsel[:, :, :], AX.X, ALU.add))
                ch.wait()
                ch.mark(nc.vector.tensor_tensor(resi[:, :], dsum[:, :], posf[:, :], ALU.add))
                dve.wait_ge(s_wts, 2 * (f + 1))
                ch.mark(nc.vector.tensor_scalar(wts[:, :, :], wts[:, :, :], 0.5, None, ALU.mult))
                ch.wait()

                def gate(t, k):
                    n = t * DUOS + k + f * PAIRS
                    dve.wait_ge(s_sig, n + 1)
                    gu = bank[2 + k % 2][:, :].rearrange("p (n w) -> p n w", n=2)
                    ch.mark(nc.vector.scalar_tensor_tensor(out=sig[:, k % 2, :, :], in0=gu[:, :, 0:F], scalar=LIMIT,
                                                           in1=sig[:, k % 2, :, :], op0=ALU.min, op1=ALU.mult))
                    ch.mark(nc.vector.tensor_scalar(upc[:, k % 2, :, :], gu[:, :, F:2 * F], LIMIT, -LIMIT, ALU.min, ALU.max))
                    ch.wait()
                    nc.vector.scalar_tensor_tensor(out=upc[:, k % 2, :, :], in0=upc[:, k % 2, :, :], scalar=1.0,
                                                   in1=sig[:, k % 2, :, :], op0=ALU.add, op1=ALU.mult).then_inc(s_gated, 1)

                ch.begin(0, 2 * DUOS)
                for k in range(DUOS):
                    gate(0, k)
                ch.end(1)
                with dve.Fori(1, TURNS) as t:
                    ch.begin(t - 1, 2 * DUOS)
                    for k in range(DUOS):
                        gate(t, k)
                ch.end(TURNS - 1)
                if f == 0:
                    continue

                def stage_rows(h, u):
                    nc.vector.tensor_copy(resg[:, u, :], resi[:, bass.ds((h * 2 + u) * (QUAD * TOPK), QUAD * TOPK)]).then_inc(s_resg[u], 1)

                def combine(h, u):
                    dve.wait_ge(s_got[u], (h + 1) * (16 * QUAD * TOPK))
                    for k in range(TOPK):
                        for i in range(QUAD):
                            t = h * (2 * QUAD) + (u * QUAD + i)
                            row = xr[:, bass.ds(t, 1), :].rearrange("p a c -> p (a c)")
                            ins = nc.vector.scalar_tensor_tensor(out=row, in0=yg[:, u, TOPK * i + k, :], scalar=wts[:, k, bass.ds(t, 1)],
                                                                 in1=row, op0=ALU.mult, op1=ALU.add)
                            if k < TOPK - 1:
                                ch.mark(ins)
                        if k < TOPK - 1:
                            ch.wait()
                    ins.then_inc(s_comb, 1)

                for u in range(2):
                    stage_rows(0, u)
                with dve.Fori(0, NQ // 2 - 1) as h:
                    ch.begin(h, 2 * QUAD)
                    for u in range(2):
                        combine(h, u)
                        stage_rows(h + 1, u)
                ch.end(NQ // 2 - 1)
                for u in range(2):
                    combine(NQ // 2 - 1, u)

        def attention_tensor(pe):
            pe.wait_ge(s_watt, 64)
            pe.wait_ge(s_asetup, 5)

            def rows_T(x):
                pe.wait_ge(a_xn, x + 1)
                for i in range(QUAD):
                    last = nc.tensor.transpose(bank[7][:, i * P:(i + 1) * P], xa[:, i, :], ident)
                last.then_inc(a_Tp, 1)

            def project(which, x):
                if which == 0:
                    pe.wait_ge(a_xT, x + 1)
                nc.tensor.matmul(bank[7][:, :], w_in[:, which * C:(which + 1) * C], xaT[:, :], start=True, stop=True).then_inc(a_made[which], 1)

            def values(x):
                for i in range(QUAD):
                    o = bank[7][:, i * C:(i + 1) * C]
                    nc.tensor.matmul(o, ones[0:3, :], bias3[:, E * EW:E * EW + C], start=True, stop=False)
                    last = nc.tensor.matmul(o, xaT[:, i * P:(i + 1) * P], w_in[:, 2 * C:3 * C], start=False, stop=True)
                last.then_inc(a_v, 1)

            def head(t, s, g):
                v, j = s // GRP, s % GRP
                r = j % 2 * HALF
                return slice(r, r + HALF), v // 2, 2 * g + j // 2, v % 2 * T

            def scores(t, s):
                n, v, j = t * UNITS + s, s // GRP, s % GRP
                if j == 0 and v % 2 == 0:
                    pe.wait_ge(a_stack[v // 2], (t + 1) * 32)
                beyond_first(pe, a_max, n)
                q, k = stack
                nc.tensor.matmul(bank[0].rearrange("p (g k) -> p g k", g=GRP), identb[:, :],
                                 mask_q[:, :].unsqueeze(1).to_broadcast([P, GRP, P]), start=True, stop=False)
                for a in range(2):
                    nc.tensor.matmul(bank[1 + a].rearrange("p (g k) -> p g k", g=2)[:, :, P:T], identb[:, :],
                                     mask_q[:, :].unsqueeze(1).to_broadcast([P, 2, P]), start=True, stop=False)
                for g in range(GRP):
                    r, pair, m, o = head(t, s, g)
                    nc.tensor.matmul(bank[0][:, g * P:(g + 1) * P], q[r, pair, m, o:o + P], k[r, pair, m, o:o + P],
                                     start=False, stop=g == GRP - 1)
                for g in range(GRP):
                    r, pair, m, o = head(t, s, g)
                    for kt in range(QT):
                        c = g % 2 * T + kt * P
                        last = nc.tensor.matmul(bank[1 + g // 2][:, c:c + P], q[r, pair, m, o + P:o + T], k[r, pair, m, o + kt * P:o + (kt + 1) * P],
                                                start=False, stop=g % 2 == 1 and kt == 1)
                last.then_inc(a_s, 1)

            def max_T(t, s):
                n = t * UNITS + s
                pe.wait_ge(a_max, n + 1)
                for qt in range(QT):
                    last = nc.tensor.matmul(bank[7][0:3 * GRP, qt * P:(qt + 1) * P], mparts[:, qt, :, :].rearrange("p a g -> p (a g)"),
                                            identb[:, :], start=True, stop=True)
                last.then_inc(a_mTp, 1)

            def weights(t, s):
                n = t * UNITS + s
                pe.wait_ge(a_mT, n + 1)
                beyond_first(pe, a_exp, n)
                q, k = stack
                for g in range(GRP):
                    nc.tensor.matmul(bank[3 + g // 2][:, g % 2 * T:(g % 2 + 1) * T], select[:, g, :], mT[:, s % 2, :], start=g % 2 == 0, stop=False)
                    nc.tensor.matmul(bank[5][:, g * P:(g + 1) * P], select[:, g, :], mT[:, s % 2, P:T], start=g == 0, stop=False)
                for a in range(2):
                    nc.tensor.matmul(bank[3 + a].rearrange("p (g k) -> p g k", g=2)[:, :, 0:P], identb[:, :],
                                     mask_k[:, :].unsqueeze(1).to_broadcast([P, 2, P]), start=False, stop=False)
                nc.tensor.matmul(bank[5].rearrange("p (g k) -> p g k", g=GRP), identb[:, :],
                                 mask_k[:, :].unsqueeze(1).to_broadcast([P, GRP, P]), start=False, stop=False)
                for g in range(GRP):
                    r, pair, m, o = head(t, s, g)
                    nc.tensor.matmul(bank[3 + g // 2][:, g % 2 * T:(g % 2 + 1) * T], k[r, pair, m, o:o + P], q[r, pair, m, o:o + T],
                                     start=False, stop=g % 2 == 1)
                for g in range(GRP):
                    r, pair, m, o = head(t, s, g)
                    last = nc.tensor.matmul(bank[5][:, g * P:(g + 1) * P], k[r, pair, m, o + P:o + T], q[r, pair, m, o + P:o + T],
                                            start=False, stop=g == GRP - 1)
                last.then_inc(a_st, 1)

            def weigh_values(t, s):
                n, v, j = t * UNITS + s, s // GRP, s % GRP
                pe.wait_ge(a_exp, n + 1)
                if j == 0:
                    pe.wait_ge(a_ysum, t * SLOTS + (v + 1))
                    if v % 2 == 0:
                        pe.wait_ge(a_vs, t * 2 + (v // 2 + 1))
                for g in range(GRP):
                    r, c = g % 2 * HALF, g // 2 * T
                    for kt in range(QT):
                        of_head = vz[:, (v * QT + kt) * GRP + g, j * HALF:(j + 1) * HALF]
                        w = pT[:, s % 2, g * T:(g + 1) * T] if kt == 0 else pT[:, s % 2, GRP * T + g * P:GRP * T + (g + 1) * P]
                        last = nc.tensor.matmul(bank[6][r:r + HALF, c + kt * P:c + T], of_head, w,
                                                start=j == 0 and g < 2 and kt == 0, stop=j == GRP - 1 and g >= 2 and kt == 1)
                last.then_inc(a_pv, 1)

            def project_out(b):
                pe.wait_ge(a_y, b + 2)
                for i in range(QT):
                    o = bank[7][:, i * C:(i + 1) * C]
                    nc.tensor.matmul(o, ones[0:3, :], bias3[:, E * EW + C:E * EW + 2 * C], start=True, stop=False)
                    last = nc.tensor.matmul(o, yT[:, i * P:(i + 1) * P], w_out[:, :], start=False, stop=True)
                last.then_inc(a_proj, 1)

            rows_T(0)
            project(0, 0)
            pe.wait_ge(a_rest[0], 1)
            project(1, 0)
            pe.wait_ge(a_rest[1], 1)
            values(0)
            pe.wait_ge(a_vs, 1)
            rows_T(1)
            scores(0, 0)
            scores(0, 1)
            pe.wait_ge(a_xT, 2)
            max_T(0, 0)

            def bank7_read(t, s):
                steps = Steps(t, s)
                for step, sem_read in ((steps.q, a_rest[0]), (steps.k, a_rest[1]), (steps.v, a_vs), (steps.x, a_xT)):
                    if step is not None:
                        pe.wait_ge(sem_read, step + 1)
                if steps.project is not None:
                    pe.wait_ge(a_x2, steps.project + 2)

            def unit(t, s):
                t0, s0 = t, s
                t, s = t + s // UNITS, s % UNITS
                n = t * UNITS + s
                steps = Steps(t, s)
                if steps.scores_next:
                    scores(*after(t, s, 2))
                if steps.max_next:
                    if s0 > 0:
                        bank7_read(*after(t0, s0 - 1, 0))
                    else:
                        pe.wait_ge(a_mT, 1)
                    max_T(*after(t, s, 1))
                weights(t, s)
                if steps.max_next:
                    pe.wait_ge(a_mT, n + 2)
                elif s0 > 0:
                    bank7_read(*after(t0, s0 - 1, 0))
                if steps.q is not None:
                    project(0, steps.q)
                if steps.k is not None:
                    project(1, steps.k)
                if steps.v is not None:
                    values(steps.v)
                if steps.x is not None:
                    rows_T(steps.x)
                if steps.project is not None:
                    project_out(steps.project)
                if s0 > 0:
                    weigh_values(*after(t0, s0 - 1, 0))

            attention_loop(pe, unit, None)
            weigh_values(TURNS_A - 1, UNITS - 1)
            bank7_read(TURNS_A - 1, UNITS - 1)
            project_out(B - 1)

        @block.tensor
        def _(pe):
            pe.wait_ge(s_const, 48)
            for f in range(2):
                if f == 1:
                    attention_tensor(pe)

                def transpose_logits(q):
                    pe.wait_ge(s_xn, f * NQ + q + 1)
                    if q >= 2:
                        pe.wait_ge(s_xnT, f * NQ + q - 1)
                    for i in range(QUAD):
                        last = nc.tensor.transpose(bank[q % 2][:, i * P:(i + 1) * P], xn[:, QUAD * q + i, :], ident)
                    last.then_inc(s_xnTp, 1)
                    pe.wait_ge(s_xnT, f * NQ + q + 1)
                    if q >= 2:
                        pe.wait_ge(s_mask, f * NQ + q - 1)
                    for i in range(QUAD):
                        last = nc.tensor.matmul(bank[2 + q % 2][:, i * E:(i + 1) * E], xnT[:, q % 2, i * P:(i + 1) * P], wg[:, :],
                                                start=True, stop=True)
                    last.then_inc(s_logit, 1)

                def ranks(q):
                    if q == 0 and f == 0:
                        pe.wait_ge(s_setup, 1)
                    pe.wait_ge(s_mask, f * NQ + q + 1)
                    if q >= 2:
                        pe.wait_ge(s_pos, f * NQ + q - 1)
                    o = bank[4 + q % 2][:, 0:QUAD * E]
                    nc.tensor.matmul(o, tri[:, :], mask[:, QUAD * q:QUAD * q + QUAD, :].rearrange("p n e -> p (n e)"), start=True, stop=False)
                    for i in range(QUAD - 1):
                        n = QUAD - 1 - i
                        nc.tensor.matmul(o[:, (i + 1) * E:].rearrange("p (n e) -> p n e", n=n), ones[:, :],
                                         mask[:, QUAD * q + i, :].unsqueeze(1).to_broadcast([P, n, E]), start=False, stop=False)
                    nc.tensor.matmul(o.rearrange("p (n e) -> p n e", n=QUAD), ones[:, :],
                                     macc[:, q, :].unsqueeze(1).to_broadcast([P, QUAD, E]), start=False, stop=True).then_inc(s_rank, 1)

                for q in range(NQ + 1):
                    if q < NQ:
                        transpose_logits(q)
                    if q >= 1:
                        ranks(q - 1)
                nc.tensor.matmul(bank[6][0:E, 0:P], macc[:, NQ, :], ones[:, :], start=True, stop=True).then_inc(s_count, 1)
                pe.wait_ge(s_ntile, f + 1)
                nc.tensor.matmul(bank[7][:, 0:2 * E], ntile[:, :], utri[:, :], start=True, stop=True).then_inc(s_cum, 1)

                pe.wait_ge(s_tab, 48 * (f + 1))
                if f == 0:
                    pe.wait_ge(s_wexp, 32)
                    pe.wait_ge(s_bias3, 80 + 48)

                held = {}

                def offsets(t, k):
                    key = (t if isinstance(t, int) else str(t), k // 2)
                    if key not in held:
                        held[key] = registers(nc, pe, tab[0:1, bass.ds(t * UNROLL + k // 2 * 4, 4)], (E - 1) * EW)
                    return held[key][k % 2 * 2:k % 2 * 2 + 2]

                def turn_x(t, k):
                    n = t * DUOS + k + f * PAIRS
                    for i in range(2):
                        pe.wait_ge(s_xt[2 * k + i], (t + 1 + f * TURNS) * 16)
                    for i in range(2):
                        last = nc.tensor.transpose(bank[k % 2][:, i * P:(i + 1) * P], xt[:, 2 * k + i, :], ident)
                    last.then_inc(s_xTp, 1)

                def gate_up(t, k):
                    n = t * DUOS + k + f * PAIRS
                    e = offsets(t, k)
                    pe.wait_ge(s_xT, n + 1)
                    for i in range(2):
                        o = bank[2 + k % 2][:, i * 2 * F:(i + 1) * 2 * F]
                        nc.tensor.matmul(o, ones[0:3, :], bias3[:, bass.ds(e[i], 2 * F)], start=True, stop=False)
                        last = nc.tensor.matmul(o, xT[:, k % 2, i * P:(i + 1) * P], w_all[:, bass.ds(e[i], 2 * F)],
                                                start=False, stop=True)
                    last.then_inc(s_gu, 1)

                def turn_g(t, k):
                    n = t * DUOS + k + f * PAIRS
                    pe.wait_ge(s_gated, n + 1)
                    for i in range(2):
                        last = nc.tensor.transpose(bank[4 + k % 2][:, i * P:(i + 1) * P], upc[:, k % 2, i, :], ident)
                    last.then_inc(s_gTp, 1)

                def down(t, k):
                    n = t * DUOS + k + f * PAIRS
                    e = offsets(t, k)
                    pe.wait_ge(s_gT, n + 1)
                    beyond_first(pe, s_ysb, n - 1)
                    for i in range(2):
                        o = bank[6 + k % 2][:, i * C:(i + 1) * C]
                        nc.tensor.matmul(o, ones[0:3, :], bias3[:, bass.ds(e[i] + 2 * F, C)], start=True, stop=False)
                        last = nc.tensor.matmul(o, gT[:, k % 2, i * P:(i + 1) * P], w_all[:, bass.ds(e[i] + 2 * F, C)],
                                                start=False, stop=True)
                    last.then_inc(s_y, 1)

                expert_pipeline(pe, turn_x, gate_up, turn_g, down)


class Steps:

    def __init__(self, t, s):
        v, j = s // GRP, s % GRP
        b = t * SLOTS + v
        last = isinstance(t, int) and t == TURNS_A - 1
        half = v // 2
        self.half = 1 - half

        def pair(ahead):
            x = t * 2 + half + ahead
            return x if not isinstance(x, int) or x < B // 2 else None

        self.scores_next = not last or s + 2 < UNITS
        self.max_next = not last or s + 1 < UNITS
        self.q = self.k = self.v = self.x = self.sums = self.project = None
        self.divide = self.add = self.combine = self.name = self.normalise = None
        if v % 2 == 0:
            if j == 0:
                self.q = pair(1)
            if j == 1:
                self.k, self.name = pair(1), pair(2)
            if j == 3:
                self.combine = pair(2)
        else:
            if j == 0:
                self.v, self.normalise = pair(1), pair(2)
            if j == 1:
                self.x = pair(2)
        if j == 0 and (not isinstance(b, int) or b > 0):
            self.sums = b - 1
        if j == 1:
            self.divide = b - 1
        if j == 3:
            self.project = self.add = b - 1


def after(t, s, ahead):
    return t + (s + ahead) // UNITS, (s + ahead) % UNITS


def attention_loop(eng, unit, chain):
    unit(0, 0)
    with eng.Fori(0, TURNS_A - 1) as t:
        if chain:
            chain[0].begin(t, chain[1])
        for s in range(1, UNITS + 1):
            unit(t, s)
    if chain:
        chain[0].end(TURNS_A - 1)
    for s in range(1, UNITS):
        unit(TURNS_A - 1, s)


ATT_CHAIN = 120


def registers(nc, eng, table, most):
    return nc.values_load_multi_w_load_instructions(table, engines=[eng.engine], min_val=0, max_val=most,
                                                    skip_runtime_bounds_check_because="the table is made on the chip")[1]


def beyond_first(eng, sem, value):
    if not isinstance(value, int) or value > 0:
        eng.wait_ge(sem, value)


def expert_pipeline(eng, first, second, third, fourth):
    steps = (first, second, third, fourth)

    def slot(t, k, from_turn, to_turn):
        for behind, step in enumerate(steps):
            pair = k - behind
            turn, k2 = t + pair // DUOS, pair % DUOS
            if isinstance(turn, int) and not from_turn <= turn < to_turn:
                continue
            step(turn, k2)

    def turn(t):
        for k in range(DUOS):
            slot(t, k, 0, TURNS)

    turn(0)
    turn(1)
    with eng.Fori(2, TURNS) as t:
        turn(t)
    for k in range(len(steps) - 1):
        slot(TURNS, k, 0, TURNS)


_OUT = (B, T, C)


def kernel(**inputs):
    import concourse.bacc as bacc
    from concourse.bass_utils import run_bass_kernel_spmd

    w = {k: np.asarray(v) for k, v in inputs.items()}
    parts = {
        "x": w["L0_attn_x"].reshape(N, C),
        "w_g": w["L0_ffn_Wg"].T,
        "b_g": w["L0_ffn_bg"],
        "w_gu": w["L0_ffn_Wgu"].reshape(E, C, F, 2).transpose(1, 0, 3, 2).reshape(C, E * 2 * F),
        "w_d": w["L0_ffn_Wd"].transpose(1, 0, 2).reshape(F, E * C),
        "b_gu": w["L0_ffn_bgu"].reshape(E, F, 2).transpose(0, 2, 1).reshape(E, 2 * F),
        "b_d": w["L0_ffn_bd"],
        "b_attn": w["L0_attn_b_attn"].reshape(3, C),
        "b_proj": w["L0_attn_b_proj"].reshape(1, C),
        "w_attn": w["L0_attn_W_attn"],
        "w_proj": w["L0_attn_W_proj"],
        "konst": shape_constants(),
    }
    nc = bacc.Bacc("TRN2", target_bir_lowering=False, num_devices=1)
    arrays, aps = {}, {}
    for name, a in parts.items():
        arrays[f"in_{name}"] = np.ascontiguousarray(a)
        aps[name] = nc.dram_tensor(f"in_{name}", a.shape, mybir.dt.from_np(a.dtype), kind="ExternalInput").ap()
    out = nc.dram_tensor("out", (N, C), F32, kind="ExternalOutput").ap()
    build_block(nc, out=out, **aps)
    r = run_bass_kernel_spmd(nc, [arrays], core_ids=[0])
    return r.results[0]["out"].reshape(_OUT)
```

```python
from contextlib import ExitStack

import numpy as np

import concourse.bass as bass
from concourse import mybir

F32 = mybir.dt.float32
F32R = mybir.dt.float32r
BF16 = mybir.dt.bfloat16
I32 = mybir.dt.int32
U32 = mybir.dt.uint32
ALU = mybir.AluOpType
ACT = mybir.ActivationFunctionType
AX = mybir.AxisListType

P = 128
B, T, C = 16, 256, 128
N = B * T
NT = N // P
QUAD = 4
NQ = NT // QUAD
EARLY = 2
MERGED = NQ - 2
E, TOPK, F = 16, 2, 128
ROW = C + 1
REGION = N + P
TILES = N * TOPK // P + E
UNROLL = 8
DUOS = UNROLL // 2
TURNS = TILES // UNROLL
ALPHA, LIMIT, EPS = 1.702, 7.0, 1e-5
ROUND = 1.5 * 2.0 ** 23
EW = 2 * F + C
NEG = -1e30
H, D = 16, 8
SCALE = D ** -0.5
GRP = 4
QT = T // P
HALF = P // 2
PARTS = HALF // D
ROWS_V = HALF + D
SLOTS = 4
UNITS = SLOTS * GRP
TURNS_A = B // SLOTS

K_ID, K_TRI = 0, 128
K_E, K_BASE, K_ROW, K_ROW128, K_BASEP = 256, 272, 288, 289, 290
K_U = 291
K_MQ, K_MK = 323, 451
K_SEL = 579
K_EW = K_SEL + GRP * P
K_NUM = K_EW + E
K_NONE = K_NUM + NT * TOPK
K_W = K_NONE + TILES


def shape_constants():
    p = np.arange(P)
    k = np.zeros((P, K_W), np.float32)
    k[:, K_ID:K_ID + P] = np.eye(P)
    k[:, K_TRI:K_TRI + P] = p[:, None] < p[None, :]
    k[:, K_E:K_E + E] = np.arange(E)
    k[:, K_EW:K_EW + E] = np.arange(E) * EW
    k[:, K_NUM:K_NUM + NT * TOPK] = ((np.arange(NT)[None, :, None] * P + p[:, None, None]) * TOPK + np.arange(TOPK)).reshape(P, -1)
    k[:, K_NONE:K_NONE + TILES] = N * TOPK + np.arange(TILES)[None, :] * P + p[:, None]
    k[:, K_BASE:K_BASE + E] = P + np.arange(E) * REGION
    k[:, K_ROW] = p
    k[:, K_ROW128] = p * P
    k[:, K_BASEP] = P + p * REGION
    e = np.arange(E)
    k[:E, K_U:K_U + E] = e[:, None] <= e[None, :]
    k[:E, K_U + E:K_U + 2 * E] = e[:, None] < e[None, :]
    k[:, K_MQ:K_MQ + P] = np.where(p[None, :] > p[:, None], NEG, 0)
    k[:, K_MK:K_MK + P] = np.where(p[:, None] > p[None, :], NEG, 0)
    for g in range(GRP):
        for part in range(3):
            k[part * GRP + g, K_SEL + g * P:K_SEL + (g + 1) * P] = 1
    return k


class Chain:

    def __init__(self, eng, sem):
        self.eng, self.sem, self.count, self.turns = eng, sem, 0, 0

    def mark(self, ins):
        ins.then_inc(self.sem, 1)
        self.count += 1
        return self.count + self.turns

    def wait(self, value=None):
        self.eng.wait_ge(self.sem, self.count + self.turns if value is None else value)

    def begin(self, turn, per_turn):
        self.start, self.per_turn = self.count, per_turn
        self.turns = turn * per_turn

    def end(self, turns):
        assert self.count - self.start == self.per_turn, (self.count - self.start, self.per_turn)
        self.count = self.start + turns * self.per_turn
        self.turns = 0


def build_block(nc, x, w_g, b_g, w_gu, w_d, b_gu, b_d, b_attn, b_proj, w_attn, w_proj, konst, out):
    ctx = ExitStack()
    with ctx:
        def sb(name, shape, dt=F32):
            return ctx.enter_context(nc.sbuf_tensor(name, shape, dt))

        def sem(name):
            return ctx.enter_context(nc.semaphore(name))

        banks = ctx.enter_context(nc.psum_tensor("banks", [P, 8, 512], F32))
        bank = [banks[:, i, :] for i in range(8)]

        rows_dram = nc.dram_tensor("rows_by_expert", (P + E * REGION, ROW), F32, kind="Internal").ap()
        stack_dram = [[nc.dram_tensor(f"{n}_by_part{i}", (P, PARTS, QUAD * P), BF16, kind="Internal").ap() for i in range(2)] for n in "qk"]
        results_dram = nc.dram_tensor("results_by_token", ((N * TOPK + TILES * P), C), F32, kind="Internal").ap()

        xs = sb("x_resident", [P, QT + NT, C])
        xr = xs[:, QT:, :]
        kc = sb("konst_sb", [P, K_W])
        ident = kc[:, K_ID:K_ID + P]
        tri = sb("tri", [P, P], BF16)
        ones = sb("ones", [P, P], BF16)
        utri = sb("utri", [E, 2 * E], BF16)
        wg = sb("wg", [P, E])
        bg = sb("bg", [P, E])
        w_all = sb("w_experts", [P, E * EW])
        zeros = sb("zeros", [P, ROW])
        NB = E + 1
        bias_in = sb("bias_in", [NB, EW])
        bias_hi = sb("bias_hi", [NB, EW], BF16)
        bias_mid = sb("bias_mid", [NB, EW], BF16)
        bias_lo = sb("bias_lo", [NB, EW], BF16)
        bias3 = sb("bias3", [3, NB * EW], BF16)

        vz = sb("values_spread", [P, SLOTS * QT * GRP, GRP * ROWS_V])
        rows = vz.rearrange("p a w -> p (a w)")[:, 0:NT * TOPK * ROW].rearrange("p (n k c) -> p n k c", n=NT, k=TOPK)
        st6 = sb("st6", [P, NT, 6])
        mv = sb("mv", [P, NT, 2])
        veps = sb("veps", [P, NT])
        rstd = sb("rstd", [P, NT])
        neghalf = sb("neghalf", [P, NT])
        xnT = sb("xnT", [P, 2, QUAD * P])
        lg = sb("lg", [P, NQ, QUAD, E])
        mx = sb("mx", [P, NT, 8])
        mi = sb("mi", [P, NT, 8], U32)
        mif = sb("mif", [P, NT, TOPK])
        oh = sb("oh", [P, NT, TOPK, E], BF16)
        mask = sb("mask", [P, NT, E], BF16)
        macc = sb("macc", [P, NQ + 1, E], BF16)
        msum = sb("msum", [P, NQ, E])
        gap = sb("gap", [P, NT])
        rank = sb("rank", [P, NQ, QUAD, E])
        rsel = sb("rsel", [P, NQ, QUAD * TOPK, E])
        posf = sb("posf", [P, NT * TOPK])
        posi = sb("posi", [P, NT * TOPK], I32)
        wts = sb("wts", [P, TOPK, NT])
        cnt = sb("cnt", [E, P])
        cntr = sb("cntr", [E, P])
        ntile = sb("ntile", [E, P], BF16)
        cum = sb("cum", [P, 2 * E])
        delta = sb("delta", [P, E])
        below = sb("below", [P, 2 * E])
        hot = sb("hot", [P, E])
        rowof = sb("rowof", [P, E])
        tmp2 = sb("tmp2", [P, 2, E])
        tabf = sb("tabf", [P, 2])
        tabc = sb("tabc", [P, 2], I32)
        zrow = sb("zrow", [E, 1], I32)
        tab = sb("tab", [1, 2 * TILES + E], I32)
        xt = sb("xt", [P, UNROLL, ROW])
        goes_to = sb("goes_to", [P, UNROLL], I32)
        xT = sb("xT", [P, 2, 2 * P])
        sig = sb("sig", [P, 2, 2, F])
        upc = sb("upc", [P, 2, 2, F])
        gT = sb("gT", [P, 2, 2 * P])
        ysb_rows = sb("ysb", [P, QUAD * TOPK * ROW])
        ysb = ysb_rows[:, 0:UNROLL * C].rearrange("p (k i c) -> p k i c", k=DUOS, i=2)
        w_in = sb("w_attn_sb", [P, 3 * C])
        w_out = sb("w_proj_sb", [P, C])
        bqk = sb("bqk", [P, 2])
        identb = sb("identb", [P, P], BF16)
        mask_q = sb("mask_q", [P, P], BF16)
        mask_k = sb("mask_k", [P, P], BF16)
        select = sb("select", [3 * GRP, GRP, P], BF16)
        a_st6 = sb("a_st6", [P, QUAD, 6])
        a_mv = sb("a_mv", [P, QUAD, 2])
        a_ve = sb("a_ve", [P, QUAD])
        a_rs = sb("a_rs", [P, QUAD])
        xa = xnT[:, 0, :].rearrange("p (n c) -> p n c", n=QUAD)
        xaT = xnT[:, 1, :]
        parts = [sb(f"{n}_parts", [P, 3, QUAD * P], BF16) for n in "qk"]
        rest = [buf.rearrange("p a n f -> p (a n f)") for buf in (sig, upc)]
        stack = [sb(f"{n}_stack", [P, SLOTS // 2, H // 2, QUAD * P], BF16) for n in "qk"]
        mraw = sb("mraw", [P, QT, GRP])
        mrest = sb("mrest", [P, QT, GRP])
        mparts = sb("mparts", [P, QT, 3, GRP], BF16)
        mT = sb("mT", [3 * GRP, 2, QT * P], BF16)
        pT = sb("pT", [P, 2, 3 * GRP * P])
        ysum = sb("ysum", [P, QT * 2 * P])
        rsum = sb("rsum", [P, QT * 2 * P])
        yT = sb("yT", [P, QT * P])
        spare = sb("spare", [P, 1])
        yg_rows = sb("yg", [P, QUAD * TOPK, ROW])
        a_yg = yg_rows.rearrange("p n c -> p (n c)")[:, 0:QUAD * TOPK * C].rearrange("p (n c) -> p n c", c=C)
        row_bufs = [buf.rearrange("p (n k) c -> p n k c", k=TOPK) for buf in (xt, yg_rows, sb("row_buf", [P, QUAD * TOPK, ROW]))]
        row_bufs.append(ysb_rows.rearrange("p (n k c) -> p n k c", n=QUAD, k=TOPK))
        BUFS = len(row_bufs)

        def merged(f, q):
            return f == 1 and q < MERGED

        def rows_of(f, q):
            return row_bufs[q % BUFS] if merged(f, q) else rows[:, QUAD * q:QUAD * q + QUAD, :, :]

        def xnT_of(f, q):
            return xT.rearrange("p a c -> p (a c)") if merged(f, q) else xnT[:, q % 2, :]

        def logits_bank(f, q):
            return bank[7][:, 0:QUAD * E] if merged(f, q) else bank[2 + q % 2][:, 0:QUAD * E]

        def ranks_bank(f, q):
            return bank[7][:, QUAD * E:2 * QUAD * E] if merged(f, q) else bank[4 + q % 2][:, 0:QUAD * E]

        def router_step(s, unit_of_first):
            q, odd = divmod(s - unit_of_first, 2)
            return q if not odd and 0 <= q < MERGED else None

        def read_until(s):
            return sum(2 * q + first <= s for q in range(MERGED) for first in (3, 5))
        last_results = vz.rearrange("p a w -> p (a w)")[:, 0:NT * TOPK * C].rearrange("p (n c) -> p n c", n=NT)

        s_const = sem("s_const")
        s_wexp = sem("s_wexp")
        s_x = [sem(f"s_x{i}") for i in range(NQ)]
        s_bias3 = sem("s_bias3")
        s_setup = sem("s_setup")
        s_vec = sem("s_vec")
        s_act = sem("s_act")
        s_pool = sem("s_pool")
        s_veps = sem("s_veps")
        s_rstd = sem("s_rstd")
        s_xn = sem("s_xn")
        s_xnTp = sem("s_xnTp")
        s_xnT = sem("s_xnT")
        s_logit = sem("s_logit")
        s_mask = sem("s_mask")
        s_rank = sem("s_rank")
        s_pos = sem("s_pos")
        s_scat = sem("s_scat")
        s_count = sem("s_count")
        s_ntile = sem("s_ntile")
        s_cum = sem("s_cum")
        s_table = sem("s_table")
        s_tab = sem("s_tab")
        s_ends = sem("s_ends")
        s_tab_ends = sem("s_tab_ends")
        s_zero = sem("s_zero")
        s_wts = sem("s_wts")
        s_xt = [sem(f"s_xt{i}") for i in range(UNROLL)]
        s_xTp = sem("s_xTp")
        s_goes = sem("s_goes")
        s_xT = sem("s_xT")
        s_gu = sem("s_gu")
        s_sig = sem("s_sig")
        s_gated = sem("s_gated")
        s_gTp = sem("s_gTp")
        s_gT = sem("s_gT")
        s_y = sem("s_y")
        s_ysb = [sem(f"s_ysb{k}") for k in range(DUOS)]
        s_store = [sem(f"s_store{k}") for k in range(DUOS)]
        s_got = [sem(f"s_got{i}") for i in range(NQ)]
        s_comb = sem("s_comb")
        s_out = sem("s_out")
        s_watt = sem("s_watt")
        s_asetup = sem("s_asetup")
        s_number = sem("s_number")
        s_copy = sem("s_copy")
        s_read = sem("s_read")
        s_buf = [sem(f"s_buf{i}") for i in range(4)]
        a_comb = sem("a_comb")
        a_mid = sem("a_mid")
        a_got = sem("a_got")
        a_veps = sem("a_veps")
        a_rstd = sem("a_rstd")
        a_xn = sem("a_xn")
        a_Tp = sem("a_Tp")
        a_xT = sem("a_xT")
        a_made = [sem(f"a_{n}_made") for n in "qk"]
        a_high = [sem(f"a_{n}_high") for n in "qk"]
        a_rest = [sem(f"a_{n}_rest") for n in "qk"]
        a_low = [sem(f"a_{n}_low") for n in "qk"]
        a_spread = [sem(f"a_{n}_spread") for n in "qk"]
        a_v = sem("a_v")
        a_vs = sem("a_vs")
        a_s = sem("a_s")
        a_max = sem("a_max")
        a_mTp = sem("a_mTp")
        a_mT = sem("a_mT")
        a_st = sem("a_st")
        a_exp = sem("a_exp")
        a_pv = sem("a_pv")
        a_ysum = sem("a_ysum")
        a_y = sem("a_y")
        s_vz = sem("s_vz")
        a_proj = sem("a_proj")
        a_x2 = sem("a_x2")
        a_stack = [sem(f"a_stack{i}") for i in range(2)]

        x_t = x.rearrange("(n p) c -> p n c", p=P)
        out_t = out.rearrange("(n p) c -> p n c", p=P)
        results_t = results_dram[0:N * TOPK, :].rearrange("(n p k) c -> p n (k c)", p=P, k=TOPK)
        PAIRS = TILES // 2

        block = ctx.enter_context(nc.Block())

        def stack_all(sp):
            def stack_pair(turn, half):
                x = turn * 2 + half
                first = isinstance(x, int)
                scored = None if first else sp.snap(x * 8 - 8)
                for which in range(2):
                    sp.wait_ge(a_low[which], x + 1)
                    if which == 0 and not first:
                        sp.wait_ge(a_st, scored)
                    src, dst = parts[which], stack_dram[which][half]
                    if which == 0:
                        for a in range(2):
                            sp.dma_start(dst[:, 3 * a:3 * a + 3, :], src[:, a:a + 1, :].to_broadcast([P, 3, QUAD * P])).then_inc(a_spread[0], 16)
                        sp.dma_start(dst[:, 6:8, :], src[:, 2:3, :].to_broadcast([P, 2, QUAD * P])).then_inc(a_spread[0], 16)
                    else:
                        for a in range(2):
                            sp.dma_start(dst[:, 3 * a:3 * a + 3, :], src[:, :, :]).then_inc(a_spread[1], 16)
                        sp.dma_start(dst[:, 6:8, :], src[:, 0:2, :]).then_inc(a_spread[1], 16)
                for which in range(2):
                    sp.wait_ge(a_spread[which], x * 48 + 48)
                    sp.dma_start(stack[which][:, half, :, :], stack_dram[which][half].rearrange("(m r) p t -> (r p) m t", m=H // 2)).then_inc(a_stack[half], 16)

            for half in range(2):
                stack_pair(0, half)
            with sp.Fori(1, TURNS_A) as t:
                for half in range(2):
                    stack_pair(t, half)

        def zero_tiles(eng, half):
            with eng.Fori(0, E // 8) as e:
                for r in registers(nc, eng, tab[0:1, bass.ds(e * 4 + (2 * TILES + half * E // 2), 4)], E * REGION):
                    eng.dma_start(rows_dram[bass.ds(r, P), :], zeros[:, :]).then_inc(s_zero, 16)

        @block.sync
        def _(sp):
            sp.dma_start(xr[:, 0:QUAD, :], x_t[:, 0:QUAD, :]).then_inc(s_x[0], 16)
            sp.dma_start(kc[:, :], konst).then_inc(s_const, 16)
            sp.dma_start(wg[:, :], w_g).then_inc(s_const, 16)
            sp.dma_start(bg[:, :], b_g.partition_broadcast(P)).then_inc(s_const, 16)
            for q in range(1, NQ):
                sp.dma_start(xr[:, QUAD * q:QUAD * q + QUAD, :], x_t[:, QUAD * q:QUAD * q + QUAD, :]).then_inc(s_x[q], 16)
            sp.dma_start(bias_in[0:E, 0:2 * F], b_gu).then_inc(s_bias3, 16)
            sp.dma_start(bias_in[0:E, 2 * F:EW], b_d).then_inc(s_bias3, 16)
            sp.dma_start(bias_in[E:NB, 0:C], b_attn[2:3, :]).then_inc(s_bias3, 16)
            sp.dma_start(bias_in[E:NB, C:2 * C], b_proj).then_inc(s_bias3, 16)
            sp.dma_start(bias_in[E:NB, 2 * C:EW], b_proj).then_inc(s_bias3, 16)
            w_of_expert = w_all.rearrange("p (e w) -> p e w", e=E)
            sp.dma_start(w_of_expert[:, :, 0:2 * F], w_gu.rearrange("p (e w) -> p e w", e=E)).then_inc(s_wexp, 16)
            sp.dma_start(w_of_expert[:, :, 2 * F:EW], w_d.rearrange("p (e w) -> p e w", e=E)).then_inc(s_wexp, 16)
            sp.wait_ge(s_setup, 2)
            for r, part in enumerate((bias_hi, bias_mid, bias_lo)):
                sp.dma_start(bias3[r:r + 1, :].rearrange("a (e w) -> a e w", e=NB), part[:, :]).then_inc(s_bias3, 16)

            sp.dma_start(w_in[:, :], w_attn).then_inc(s_watt, 16)
            sp.dma_start(w_out[:, :], w_proj).then_inc(s_watt, 16)
            for i in range(2):
                sp.dma_start(bqk[:, i:i + 1], b_attn[i:i + 1, :].rearrange("a c -> c a")).then_inc(s_watt, 16)

            for f in range(2):
                if f == 1:
                    stack_all(sp)
                sp.wait_ge(s_ends, f + 1)
                sp.dma_start(tab[0:1, 2 * TILES:2 * TILES + E], zrow[:, :]).then_inc(s_tab_ends, 16)
                sp.wait_ge(s_tab_ends, 16 * (f + 1))
                if f == 0:
                    sp.wait_ge(s_pool, 1)
                    sp.wait_ge(s_number, 1)
                    sp.dma_start(rows_dram[0:P, :], zeros[:, :]).then_inc(s_zero, 16)
                zero_tiles(sp, 0)
                sp.wait_ge(s_table, 1 + f)
                for k in range(2):
                    sp.dma_start(tab[0:1, k * TILES:(k + 1) * TILES], tabc[0:TILES, k:k + 1]).then_inc(s_tab, 16)
                sp.wait_ge(s_tab, 32 * (f + 1))
                sp.wait_ge(s_zero, 16 * (1 + E * (f + 1)))
                sp.wait_ge(s_scat, 16 * TOPK * (NT + f * (NT - MERGED * QUAD)))
                if f == 1:
                    for i, done in enumerate(s_buf):
                        sp.wait_ge(done, 16 * QUAD * TOPK * len(range(i, MERGED, BUFS)))

                def rows_of_tiles(turn, u):
                    return registers(nc, sp, tab[0:1, bass.ds(turn * UNROLL + (TILES + u), 4)], E * REGION)

                def load_tile(r, u):
                    sp.dma_start(xt[:, u, :], rows_dram[bass.ds(r, P), :]).then_inc(s_xt[u], 16)

                for u in range(0, UNROLL, 4):
                    for i, r in enumerate(rows_of_tiles(0, u)):
                        load_tile(r, u + i)
                with sp.Fori(1, TURNS) as t:
                    for k in range(DUOS):
                        sp.wait_ge(s_goes, t * DUOS + (k + 1 - DUOS) + f * PAIRS)
                        if k % 2 == 0:
                            rows = rows_of_tiles(t, 2 * k)
                        for i in range(2):
                            load_tile(rows[k % 2 * 2 + i], 2 * k + i)
            for k in range(DUOS):
                sp.wait_ge(s_store[k], 32 * TURNS * 2)
            for q in range(1, NQ, 2):
                sp.dma_start(last_results[:, q * QUAD:(q + 1) * QUAD, :], results_t[:, q * QUAD:(q + 1) * QUAD, :]).then_inc(s_got[q], 16)
            for q in range(NQ):
                sp.wait_ge(s_comb, q + 1)
                sp.dma_start(out_t[:, QUAD * q:QUAD * q + QUAD, :], xr[:, QUAD * q:QUAD * q + QUAD, :]).then_inc(s_out, 16)
            sp.wait_ge(s_out, 16 * NQ)

        @block.gpsimd
        def _(pool):
            nc.gpsimd.memset(zeros[:, 0:C], 0.0).then_inc(s_pool, 1)
            nc.gpsimd.memset(neghalf[:, :], -0.5).then_inc(s_pool, 1)
            pool.wait_ge(s_pool, 2)
            for f in range(2):
                if f == 1:
                    def load_results(x):
                        pool.dma_start(a_yg.rearrange("p (n k) c -> p n (k c)", n=QUAD), results_t[:, bass.ds(x * QUAD, QUAD), :]).then_inc(a_got, 16)

                    def root_of_pair(x):
                        pool.wait_ge(a_veps, x)
                        nc.gpsimd.tensor_tensor(a_rs[:, :], a_ve[:, :], neghalf[:, 0:QUAD], ALU.pow).then_inc(a_rstd, 1)

                    def parts_of_pair(x):
                        for which in range(2):
                            pool.wait_ge(s_pool, 2)
                            pool.wait_ge(a_rest[which], x)
                            nc.gpsimd.tensor_copy(parts[which][:, 1, :], rest[which][:, :]).then_inc(a_mid, 1)
                            pool.wait_ge(a_mid, x * 2 + (which - 3))
                            nc.gpsimd.tensor_tensor(parts[which][:, 2, :], rest[which][:, :], parts[which][:, 1, :],
                                                    ALU.subtract).then_inc(a_low[which], 1)

                    load_results(0)
                    pool.wait_ge(a_comb, 1)
                    load_results(1)
                    root_of_pair(1)
                    with pool.Fori(2, B // 2) as x:
                        pool.wait_ge(a_comb, x)
                        load_results(x)
                        root_of_pair(x)
                        parts_of_pair(x)
                    root_of_pair(B // 2)
                    parts_of_pair(B // 2)

                def root(group, lo, hi):
                    pool.wait_ge(s_veps, f * 2 + group + 1)
                    ts = slice(lo * QUAD, hi * QUAD)
                    nc.gpsimd.tensor_tensor(rstd[:, ts], veps[:, ts], neghalf[:, ts], ALU.pow).then_inc(s_rstd, 1)

                def scatter(q):
                    pool.wait_ge(s_pos, f * NQ + q + 1)
                    pool.wait_ge(s_copy, f * NQ + q + 1)
                    for i in range(QUAD):
                        for k in range(TOPK):
                            c = (QUAD * q + i) * TOPK + k
                            pool.indirect_dma_start(
                                out=rows_dram, out_offset=bass.IndirectOffsetOnAxis(ap=posi[:, c:c + 1], axis=0),
                                in_=rows_of(f, q)[:, i, k, :], in_offset=None).then_inc(s_buf[q % BUFS] if merged(f, q) else s_scat, 16)

                if f == 0:
                    root(0, 0, EARLY)
                    scatter(0)
                    root(1, EARLY, NQ)
                    for q in range(1, NQ):
                        scatter(q)
                else:
                    for group in range(MERGED // 2):
                        root(group, 2 * group, 2 * group + 2)
                    for q in range(MERGED - 1):
                        scatter(q)
                    root(MERGED // 2, MERGED, NQ)
                    for q in range(MERGED - 1, NQ):
                        scatter(q)

                if f == 0:
                    pool.wait_ge(s_scat, 16 * NT * TOPK)
                    nc.gpsimd.memset(vz[:, :, :], 0.0).then_inc(s_pool, 1)
                    pool.wait_ge(s_pool, 3)
                    nc.gpsimd.memset(vz[:, :, :].rearrange("p a (j w) -> p a j w", j=GRP)[:, :, :, P // 4:P // 4 + D], 1.0).then_inc(s_vz, 1)
                with pool.Fori(f * TURNS + 1, (f + 1) * TURNS + 1) as t:
                    for k in range(DUOS):
                        pool.wait_ge(s_pool, 2)
                        pool.wait_ge(s_ysb[k], t)
                        for i in range(2):
                            pool.indirect_dma_start(
                                out=results_dram, out_offset=bass.IndirectOffsetOnAxis(ap=goes_to[:, 2 * k + i:2 * k + i + 1], axis=0),
                                in_=ysb[:, k, i, :], in_offset=None).then_inc(s_store[k], 16)

                for k in range(DUOS):
                    pool.wait_ge(s_store[k], 32 * TURNS * (f + 1))

        def attention_scalar(act, router):
            def evac_xT(x):
                act.wait_ge(a_Tp, x + 1)
                nc.scalar.activation(xaT[:, :], bank[7][:, :], ACT.Identity).then_inc(a_xT, 1)

            def high(which, x):
                act.wait_ge(a_made[which], x + 1)
                beyond_first(act, a_spread[which], x * 48)
                nc.scalar.activation(parts[which][:, 0, :], bank[7][:, :], ACT.Identity, bias=bqk[:, which:which + 1]).then_inc(a_high[which], 1)

            def evac_v(x, half):
                act.wait_ge(a_v, x + 1)
                to = vz[:, half * 2 * QT * GRP:(half + 1) * 2 * QT * GRP, :].rearrange("p a (j w) -> p a j w", j=GRP)
                nc.scalar.activation(to[:, :, :, 0:D], bank[7][:, :].rearrange("p (a j d) -> p a j d", j=GRP, d=D), ACT.Identity).then_inc(a_vs, 1)

            def evac_max(t, s):
                n = t * UNITS + s
                act.wait_ge(a_mTp, n + 1)
                beyond_first(act, a_st, n - 1)
                nc.scalar.activation(mT[:, s % 2, :], bank[7][0:3 * GRP, 0:QT * P], ACT.Identity, scale=-1.0).then_inc(a_mT, 1)

            def exp(t, s):
                n = t * UNITS + s
                act.wait_ge(a_st, n + 1)
                nc.scalar.activation(pT[:, s % 2, :],
                                     banks[:, 3:6, :].rearrange("p a q -> p (a q)"), ACT.Exp, scale=SCALE).then_inc(a_exp, 1)

            def evac_sums(b):
                act.wait_ge(a_pv, (b + 1) * GRP)
                act.wait_ge(a_y, b * 2 + 2)
                nc.scalar.activation(ysum[:, :], bank[6][:, :], ACT.Identity).then_inc(a_ysum, 1)

            act.wait_ge(s_vz, 1)
            evac_xT(0)
            high(0, 0)
            high(1, 0)
            evac_v(0, 0)
            evac_xT(1)
            evac_max(0, 0)

            def unit(t, s):
                t, s = t + s // UNITS, s % UNITS
                steps = Steps(t, s)
                if steps.max_next:
                    evac_max(*after(t, s, 1))
                exp(t, s)
                if steps.q is not None:
                    high(0, steps.q)
                if steps.k is not None:
                    high(1, steps.k)
                if steps.v is not None:
                    evac_v(steps.v, steps.half)
                if steps.x is not None:
                    evac_xT(steps.x)
                if steps.sums is not None:
                    evac_sums(steps.sums)
                router(t, s)

            attention_loop(act, unit, None)
            evac_sums(B - 1)

        @block.scalar
        def _(act):
            for f in range(2):
                def copy_rows(q):
                    act.wait_ge(s_xn, f * NQ + q + 1)
                    nc.scalar.activation(rows_of(f, q)[:, :, 1, 0:C], rows_of(f, q)[:, :, 0, 0:C], ACT.Identity).then_inc(s_copy, 1)

                def evac_xn(q):
                    act.wait_ge(s_xnTp, f * NQ + q + 1)
                    if merged(f, q):
                        act.wait_ge(s_logit, f * NQ + q)
                    elif q >= 2:
                        act.wait_ge(s_logit, f * NQ + q - 1)
                    nc.scalar.activation(xnT_of(f, q), bank[7] if merged(f, q) else bank[q % 2], ACT.Identity).then_inc(s_xnT, 1)

                def router(t, s):
                    if isinstance(t, int) and t == TURNS_A - 1:
                        if router_step(s, 3) is not None:
                            copy_rows(router_step(s, 3))
                        if router_step(s, 2) is not None:
                            evac_xn(router_step(s, 2))

                if f == 1:
                    attention_scalar(act, router)
                for q in range(f * MERGED, NQ):
                    copy_rows(q)
                    evac_xn(q)
                act.wait_ge(s_mask, (f + 1) * NQ)
                nc.scalar.activation(wts[:, 0, :], gap[:, :], ACT.Sigmoid).then_inc(s_wts, 1)
                nc.scalar.activation(wts[:, 1, :], gap[:, :], ACT.Sigmoid, scale=-1.0).then_inc(s_wts, 1)

                act.wait_ge(s_tab_ends, 16 * (f + 1))
                if f == 0:
                    act.wait_ge(s_pool, 1)
                    act.wait_ge(s_number, 1)
                zero_tiles(act, 1)

                def evac_x(t, k):
                    n = t * DUOS + k + f * PAIRS
                    act.wait_ge(s_xTp, n + 1)
                    nc.scalar.activation(xT[:, k % 2, :], bank[k % 2][:, 0:2 * P], ACT.Identity).then_inc(s_xT, 1)

                def sigmoid(t, k):
                    n = t * DUOS + k + f * PAIRS
                    act.wait_ge(s_gu, n + 1)
                    nc.scalar.activation(sig[:, k % 2, :, :], bank[2 + k % 2][:, :].rearrange("p (n w) -> p n w", n=2)[:, :, 0:F],
                                         ACT.Sigmoid, scale=ALPHA).then_inc(s_sig, 1)

                def evac_g(t, k):
                    n = t * DUOS + k + f * PAIRS
                    act.wait_ge(s_gTp, n + 1)
                    nc.scalar.activation(gT[:, k % 2, :], bank[4 + k % 2][:, 0:2 * P], ACT.Identity).then_inc(s_gT, 1)

                def evac_y(t, k):
                    n = t * DUOS + k + f * PAIRS
                    act.wait_ge(s_y, n + 1)
                    beyond_first(act, s_store[k], (t + f * TURNS) * 32)
                    nc.scalar.activation(ysb[:, k, :, :].rearrange("p n c -> p (n c)"), bank[6 + k % 2][:, 0:2 * P],
                                         ACT.Identity).then_inc(s_ysb[k], 1)

                expert_pipeline(act, evac_x, sigmoid, evac_g, evac_y)

            for k in range(DUOS):
                act.wait_ge(s_store[k], 32 * TURNS * 2)
            for q in range(0, NQ, 2):
                act.dma_start(last_results[:, q * QUAD:(q + 1) * QUAD, :], results_t[:, q * QUAD:(q + 1) * QUAD, :]).then_inc(s_got[q], 16)

        def attention_vector(dve, ch, router):
            def row(x, i):
                return xr[:, bass.ds(x * QUAD + i, 1), :].rearrange("p a c -> p (a c)")

            def combine(x):
                dve.wait_ge(a_got, (x + 1) * 16)
                for k in range(TOPK):
                    for i in range(QUAD):
                        last = nc.vector.scalar_tensor_tensor(out=row(x, i), in0=a_yg[:, TOPK * i + k, :], scalar=wts[:, k, bass.ds(x * QUAD + i, 1)],
                                                              in1=row(x, i), op0=ALU.mult, op1=ALU.add)
                        if k < TOPK - 1:
                            ch.mark(last)
                    if k < TOPK - 1:
                        ch.wait()
                last.then_inc(a_comb, 1)

            def settle():
                ch.wait()
                ch.mark(nc.vector.memset(spare[:, :], 0.0))

            def stats(x):
                dve.wait_ge(a_comb, x + 1)
                ch.mark(nc.vector.memset(spare[:, :], 0.0))
                for i in range(QUAD):
                    ch.mark(nc.vector.bn_stats(a_st6[:, i, :], row(x, i)))
                settle()
                for i in range(QUAD):
                    ch.mark(nc.vector.bn_aggr(a_mv[:, i, :], a_st6[:, i, :]))
                ch.wait()
                nc.vector.tensor_scalar(a_ve[:, :], a_mv[:, :, 1], EPS, None, ALU.add).then_inc(a_veps, 1)

            def normalise(x):
                dve.wait_ge(a_rstd, x + 1)
                beyond_first(dve, a_Tp, x)
                for i in range(QUAD):
                    last = nc.vector.tensor_scalar(xa[:, i, :], row(x, i), a_mv[:, i, 0:1], a_rs[:, i:i + 1], ALU.subtract, ALU.mult)
                last.then_inc(a_xn, 1)

            def split_rest(which, x):
                dve.wait_ge(a_high[which], x + 1)
                beyond_first(dve, a_low[which], x)
                nc.vector.scalar_tensor_tensor(out=rest[which][:, :], in0=bank[7][:, :], scalar=bqk[:, which:which + 1],
                                               in1=parts[which][:, 0, :], op0=ALU.add, op1=ALU.subtract).then_inc(a_rest[which], 1)

            def row_max(t, s):
                n = t * UNITS + s
                dve.wait_ge(a_s, n + 1)
                beyond_first(dve, a_mTp, n)
                ch.mark(nc.vector.tensor_reduce(mraw[:, 0, :], bank[0][:, :].rearrange("p (g k) -> p g k", g=GRP), AX.X, ALU.max))
                ch.mark(nc.vector.tensor_reduce(mraw[:, 1, :], banks[:, 1:3, :].rearrange("p a (g k) -> p (a g) k", g=2), AX.X, ALU.max))
                ch.wait()
                ch.mark(nc.vector.tensor_copy(mparts[:, :, 0, :], mraw[:, :, :]))
                ch.wait()
                ch.mark(nc.vector.tensor_tensor(mrest[:, :, :], mraw[:, :, :], mparts[:, :, 0, :], ALU.subtract))
                ch.wait()
                ch.mark(nc.vector.tensor_copy(mparts[:, :, 1, :], mrest[:, :, :]))
                ch.wait()
                nc.vector.tensor_tensor(mparts[:, :, 2, :], mrest[:, :, :], mparts[:, :, 1, :], ALU.subtract).then_inc(a_max, 1)

            def divide(b, half):
                if half == 0:
                    dve.wait_ge(a_ysum, b + 2)
                c = slice(half * T, (half + 1) * T)
                ch.mark(nc.vector.reciprocal(rsum[:, c], ysum[:, c]))
                ch.wait()
                for i in range(2):
                    g, r = 2 * half + i, i * HALF
                    last = nc.vector.tensor_tensor(yT[g * 32:(g + 1) * 32, :], ysum[r:r + 32, c], rsum[r + 32:r + 64, c], ALU.mult)
                last.then_inc(a_y, 1)

            def add_attention(b):
                dve.wait_ge(a_proj, b + 2)
                rows = xs[:, bass.ds((b + 1) * QT, QT), :].rearrange("p n c -> p (n c)")
                nc.vector.tensor_tensor(rows, bank[7][:, 0:QT * C], rows, ALU.add).then_inc(a_x2, 1)

            for x in range(2):
                combine(x)
                stats(x)
                normalise(x)
                if x == 0:
                    for which in range(2):
                        split_rest(which, 0)
                        dve.wait_ge(a_rest[which], 1)
                        ch.mark(nc.vector.tensor_copy(parts[which][:, 1, :], rest[which][:, :]))
                        ch.wait()
                        nc.vector.tensor_tensor(parts[which][:, 2, :], rest[which][:, :], parts[which][:, 1, :],
                                                ALU.subtract).then_inc(a_low[which], 1)
            row_max(0, 0)
            row_max(0, 1)

            def unit(t, s):
                t, s = t + s // UNITS, s % UNITS
                steps = Steps(t, s)
                router(t, s, True)
                if steps.scores_next:
                    row_max(*after(t, s, 2))
                if steps.q is not None:
                    split_rest(0, steps.q)
                if steps.k is not None:
                    split_rest(1, steps.k)
                if steps.divide is not None:
                    divide(steps.divide, s % GRP - 1)
                if steps.add is not None:
                    add_attention(steps.add)
                if steps.combine is not None:
                    combine(steps.combine)
                    stats(steps.combine)
                if steps.normalise is not None:
                    normalise(steps.normalise)
                router(t, s, False)

            attention_loop(dve, unit, (ch, ATT_CHAIN))
            for half in range(2):
                divide(B - 1, half)
            add_attention(B - 1)

        @block.vector
        def _(dve):
            ch = Chain(dve, s_vec)
            def setup():
                dve.wait_ge(s_const, 48)
                nc.vector.tensor_copy(tri[:, :], kc[:, K_TRI:K_TRI + P]).then_inc(s_setup, 1)
                ch.mark(nc.vector.memset(ones[:, :], 1.0))
                ch.mark(nc.vector.tensor_copy(utri[:, :], kc[0:E, K_U:K_U + 2 * E]))
                ch.mark(nc.vector.memset(macc[:, :, :], 0.0))

                nc.vector.tensor_copy(identb[:, :], ident).then_inc(s_asetup, 1)
                nc.vector.tensor_copy(mask_q[:, :], kc[:, K_MQ:K_MQ + P]).then_inc(s_asetup, 1)
                nc.vector.tensor_copy(mask_k[:, :], kc[:, K_MK:K_MK + P]).then_inc(s_asetup, 1)
                nc.vector.memset(zeros[:, C:ROW], float(2 * (N * TOPK + TILES * P))).then_inc(s_number, 1)
                nc.vector.memset(ysum[:, :], 1.0).then_inc(a_ysum, 1)
                nc.vector.memset(xs[:, 0:QT, :], 0.0).then_inc(s_asetup, 1)
                nc.vector.tensor_copy(select[:, :, :].rearrange("p a k -> p (a k)"), kc[0:3 * GRP, K_SEL:K_SEL + GRP * P]).then_inc(s_asetup, 1)

            for f in range(2):
                def stats(q):
                    if f == 0:
                        dve.wait_ge(s_x[q], 16)
                    else:
                        dve.wait_ge(a_x2, 2 * q + 3)
                    for t in range(QUAD * q, QUAD * q + QUAD):
                        ch.mark(nc.vector.bn_stats(st6[:, t, :], xr[:, t, :]))
                    ch.wait()
                    for t in range(QUAD * q, QUAD * q + QUAD):
                        ch.mark(nc.vector.bn_aggr(mv[:, t, :], st6[:, t, :]))

                def variances(q0, q1):
                    ch.wait()
                    ts = slice(QUAD * q0, QUAD * q1)
                    nc.vector.tensor_scalar(veps[:, ts], mv[:, ts, 1], EPS, None, ALU.add).then_inc(s_veps, 1)

                def normalise(q):
                    if merged(f, q) and q >= BUFS:
                        dve.wait_ge(s_buf[q % BUFS], 16 * QUAD * TOPK * (q // BUFS))
                    nc.vector.tensor_copy(rows_of(f, q)[:, :, :, C], kc[:, K_NUM + q * QUAD * TOPK:K_NUM + (q + 1) * QUAD * TOPK].rearrange(
                        "p (n k) -> p n k", k=TOPK)).then_inc(s_number, 1)
                    dve.wait_ge(s_rstd, q // 2 + 3 if f == 1 else 1 if q < EARLY else 2)
                    for t in range(QUAD * q, QUAD * q + QUAD):
                        last = nc.vector.tensor_scalar(rows_of(f, q)[:, t - QUAD * q, 0, 0:C], xr[:, t, :], mv[:, t, 0:1], rstd[:, t:t + 1],
                                                       ALU.subtract, ALU.mult)
                    last.then_inc(s_xn, 1)

                reads = {}

                def read(q, what, ins):
                    if merged(f, q):
                        ins.then_inc(s_read, 1)
                        reads[what, q] = len(reads) + 1
                    else:
                        ch.mark(ins)

                def after_read(q, what):
                    if merged(f, q):
                        dve.wait_ge(s_read, reads[what, q])
                    else:
                        ch.wait()

                def read_logits(q):
                    dve.wait_ge(s_logit, f * NQ + q + 1)
                    read(q, "logits", nc.vector.tensor_tensor(lg[:, q, :, :], logits_bank(f, q).rearrange("p (n e) -> p n e", n=QUAD),
                                                              bg[:, :].unsqueeze(1).to_broadcast([P, QUAD, E]), ALU.add))

                def top2(q):
                    ts = slice(QUAD * q, QUAD * q + QUAD)
                    after_read(q, "logits")
                    for i in range(QUAD):
                        ch.mark(nc.vector.max(mx[:, QUAD * q + i, :], lg[:, q, i, :]))
                    ch.wait()
                    for i in range(QUAD):
                        ch.mark(nc.vector.max_index(mi[:, QUAD * q + i, :], mx[:, QUAD * q + i, :], lg[:, q, i, :]))
                    ch.mark(nc.vector.tensor_tensor(gap[:, ts], mx[:, ts, 0], mx[:, ts, 1], ALU.subtract))
                    ch.wait()
                    ch.mark(nc.vector.tensor_copy(mif[:, ts, :], mi[:, ts, 0:TOPK]))
                    ch.wait()
                    ch.mark(nc.vector.tensor_tensor(
                        oh[:, ts, :, :].rearrange("p n k e -> p (n k) e"),
                        kc[:, K_E:K_E + E].unsqueeze(1).to_broadcast([P, QUAD * TOPK, E]),
                        mif[:, ts, :].rearrange("p n k -> p (n k)").unsqueeze(2).to_broadcast([P, QUAD * TOPK, E]), ALU.is_equal))
                    ch.wait()
                    ch.mark(nc.vector.tensor_tensor(mask[:, ts, :], oh[:, ts, 0, :], oh[:, ts, 1, :], ALU.add))
                    ch.wait()
                    ch.mark(nc.vector.tensor_reduce(msum[:, q, :], mask[:, ts, :].rearrange("p n e -> p e n"), AX.X, ALU.add))
                    ch.wait()
                    nc.vector.tensor_tensor(macc[:, q + 1, :], macc[:, q, :], msum[:, q, :], ALU.add).then_inc(s_mask, 1)

                def read_ranks(q):
                    dve.wait_ge(s_rank, f * NQ + q + 1)
                    read(q, "ranks", nc.vector.tensor_tensor(rank[:, q, :, :], ranks_bank(f, q).rearrange("p (n e) -> p n e", n=QUAD),
                                                             kc[:, K_BASE:K_BASE + E].unsqueeze(1).to_broadcast([P, QUAD, E]), ALU.add))

                def positions(q):
                    after_read(q, "ranks")
                    for k in range(TOPK):
                        ch.mark(nc.vector.tensor_tensor(
                            rsel[:, q, :, :].rearrange("p (n k) e -> p n k e", k=TOPK)[:, :, k, :],
                            oh[:, QUAD * q:QUAD * q + QUAD, k, :], rank[:, q, :, :], ALU.mult))
                    ch.wait()
                    cs = slice(QUAD * TOPK * q, QUAD * TOPK * (q + 1))
                    ch.mark(nc.vector.tensor_reduce(posf[:, cs], rsel[:, q, :, :], AX.X, ALU.add))
                    ch.wait()
                    nc.vector.tensor_copy(posi[:, cs], posf[:, cs]).then_inc(s_pos, 1)

                def split_biases():
                    dve.wait_ge(s_bias3, 80)
                    ch.mark(nc.vector.tensor_copy(bias_hi[:, :], bias_in[:, :]))
                    ch.wait()
                    ch.mark(nc.vector.tensor_tensor(bias_in[:, :], bias_in[:, :], bias_hi[:, :], ALU.subtract))
                    ch.wait()
                    ch.mark(nc.vector.tensor_copy(bias_mid[:, :], bias_in[:, :]))
                    ch.wait()
                    ch.mark(nc.vector.tensor_tensor(bias_in[:, :], bias_in[:, :], bias_mid[:, :], ALU.subtract))
                    ch.wait()
                    nc.vector.tensor_copy(bias_lo[:, :], bias_in[:, :]).then_inc(s_setup, 1)

                def router(t, s, before):
                    if not isinstance(t, int) or t < TURNS_A - 1:
                        return
                    even = s if s % GRP == 0 else s - 1 if s % GRP == 3 else -1
                    if before:
                        if s % 2 == 1 and router_step(even, 4) is not None:
                            top2(router_step(even, 4))
                        if s % 2 == 1 and s < MERGED:
                            for q in (s - 1, s):
                                stats(q)
                            variances(s - 1, s + 1)
                        if router_step(s, 2) is not None:
                            normalise(router_step(s, 2))
                        return
                    if s % 2 == 0 and router_step(even, 4) is not None:
                        top2(router_step(even, 4))
                    if router_step(s, 5) is not None:
                        read_ranks(router_step(s, 5))
                    if router_step(s, 3) is not None:
                        read_logits(router_step(s, 3))
                    if router_step(even, 6) is not None:
                        positions(router_step(even, 6))

                if f == 0:
                    for q in range(EARLY):
                        stats(q)
                    variances(0, EARLY)
                    setup()
                    normalise(0)
                    stats(EARLY)
                    stats(EARLY + 1)
                    for q in range(NQ):
                        if q == 1:
                            for r in range(EARLY + 2, NQ):
                                stats(r)
                            variances(EARLY, NQ)
                        if q < NQ - 1:
                            normalise(q + 1)
                        read_logits(q)
                        top2(q)
                        read_ranks(q)
                        positions(q)
                        if q == 2:
                            split_biases()
                else:
                    attention_vector(dve, ch, router)
                    for q in range(MERGED, NQ):
                        stats(q)
                    variances(MERGED, NQ)
                    positions(MERGED - 1)
                    for q in range(MERGED, NQ):
                        normalise(q)
                    for q in range(MERGED, NQ):
                        read_logits(q)
                        top2(q)
                        read_ranks(q)
                        positions(q)
                dve.wait_ge(s_count, f + 1)
                nc.vector.tensor_scalar(zrow[:, :], bank[6][0:E, 0:1], kc[0:E, K_BASEP:K_BASEP + 1], None, ALU.add).then_inc(s_ends, 1)
                ch.mark(nc.vector.tensor_scalar(cnt[:, :], bank[6][0:E, 0:P], 1.0 / P, (P - 1.0) / P - 0.5 + 0.5 / P, ALU.mult, ALU.add))
                ch.wait()
                ch.mark(nc.vector.tensor_scalar(cntr[:, :], cnt[:, :], ROUND, None, ALU.add))
                ch.wait()
                nc.vector.tensor_scalar(ntile[:, :], cntr[:, :], -ROUND, None, ALU.add).then_inc(s_ntile, 1)
                dve.wait_ge(s_cum, f + 1)
                ch.mark(nc.vector.tensor_copy(cum[:, :], bank[7][:, 0:2 * E]))
                ch.wait()
                ch.mark(nc.vector.scalar_tensor_tensor(out=delta[:, :], in0=cum[:, E:2 * E], scalar=float(P),
                                                       in1=kc[:, K_BASE:K_BASE + E], op0=ALU.mult, op1=ALU.subtract))
                ch.mark(nc.vector.tensor_scalar(below[:, :], cum[:, :], kc[:, K_ROW:K_ROW + 1], None, ALU.is_le))
                ch.wait()
                ch.mark(nc.vector.tensor_tensor(hot[:, :], below[:, E:2 * E], below[:, 0:E], ALU.subtract))
                ch.mark(nc.vector.tensor_scalar(rowof[:, :], delta[:, :], -1.0, kc[:, K_ROW128:K_ROW128 + 1], ALU.mult, ALU.add))
                ch.wait()
                ch.mark(nc.vector.tensor_tensor(tmp2[:, 0, :], hot[:, :], kc[:, K_EW:K_EW + E], ALU.mult))
                ch.mark(nc.vector.tensor_tensor(tmp2[:, 1, :], hot[:, :], rowof[:, :], ALU.mult))
                ch.wait()
                ch.mark(nc.vector.tensor_reduce(tabf[:, :], tmp2[:, :, :], AX.X, ALU.add))
                ch.wait()
                nc.vector.tensor_copy(tabc[:, :], tabf[:, :]).then_inc(s_table, 1)
                dve.wait_ge(s_wts, 2 * (f + 1))
                ch.mark(nc.vector.tensor_scalar(wts[:, :, :], wts[:, :, :], 0.5, None, ALU.mult))
                ch.wait()

                def gate(t, k):
                    n = t * DUOS + k + f * PAIRS
                    beyond_first(dve, s_store[k], (t + f * TURNS) * 32)
                    dve.wait_ge(s_sig, n + 1)
                    nc.vector.tensor_tensor(goes_to[:, 2 * k:2 * k + 2], xt[:, 2 * k:2 * k + 2, C],
                                            kc[:, bass.ds(t * UNROLL + (K_NONE + 2 * k), 2)], ALU.min).then_inc(s_goes, 1)
                    gu = bank[2 + k % 2][:, :].rearrange("p (n w) -> p n w", n=2)
                    ch.mark(nc.vector.scalar_tensor_tensor(out=sig[:, k % 2, :, :], in0=gu[:, :, 0:F], scalar=LIMIT,
                                                           in1=sig[:, k % 2, :, :], op0=ALU.min, op1=ALU.mult))
                    ch.mark(nc.vector.tensor_scalar(upc[:, k % 2, :, :], gu[:, :, F:2 * F], LIMIT, -LIMIT, ALU.min, ALU.max))
                    ch.wait()
                    nc.vector.scalar_tensor_tensor(out=upc[:, k % 2, :, :], in0=upc[:, k % 2, :, :], scalar=1.0,
                                                   in1=sig[:, k % 2, :, :], op0=ALU.add, op1=ALU.mult).then_inc(s_gated, 1)

                ch.begin(0, 2 * DUOS)
                for k in range(DUOS):
                    gate(0, k)
                ch.end(1)
                with dve.Fori(1, TURNS) as t:
                    ch.begin(t - 1, 2 * DUOS)
                    for k in range(DUOS):
                        gate(t, k)
                ch.end(TURNS - 1)
                if f == 0:
                    continue

                for q in range(NQ):
                    dve.wait_ge(s_got[q], 16)
                    for k in range(TOPK):
                        for t in range(q * QUAD, (q + 1) * QUAD):
                            ins = nc.vector.scalar_tensor_tensor(out=xr[:, t, :], in0=last_results[:, t, k * C:(k + 1) * C],
                                                                 scalar=wts[:, k, t:t + 1], in1=xr[:, t, :], op0=ALU.mult, op1=ALU.add)
                            if k < TOPK - 1:
                                ch.mark(ins)
                        if k < TOPK - 1:
                            ch.wait()
                    ins.then_inc(s_comb, 1)

        def attention_tensor(pe, router):
            pe.wait_ge(s_watt, 64)
            pe.wait_ge(s_asetup, 5)

            def rows_T(x):
                pe.wait_ge(a_xn, x + 1)
                for i in range(QUAD):
                    last = nc.tensor.transpose(bank[7][:, i * P:(i + 1) * P], xa[:, i, :], ident)
                last.then_inc(a_Tp, 1)

            def project(which, x):
                if which == 0:
                    pe.wait_ge(a_xT, x + 1)
                nc.tensor.matmul(bank[7][:, :], w_in[:, which * C:(which + 1) * C], xaT[:, :], start=True, stop=True).then_inc(a_made[which], 1)

            def values(x):
                for i in range(QUAD):
                    o = bank[7][:, i * C:(i + 1) * C]
                    nc.tensor.matmul(o, ones[0:3, :], bias3[:, E * EW:E * EW + C], start=True, stop=False)
                    last = nc.tensor.matmul(o, xaT[:, i * P:(i + 1) * P], w_in[:, 2 * C:3 * C], start=False, stop=True)
                last.then_inc(a_v, 1)

            def head(t, s, g):
                v, j = s // GRP, s % GRP
                r = j % 2 * HALF
                return slice(r, r + HALF), v // 2, 2 * g + j // 2, v % 2 * T

            def scores(t, s):
                n, v, j = t * UNITS + s, s // GRP, s % GRP
                if j == 0 and v % 2 == 0:
                    pe.wait_ge(a_stack[v // 2], (t + 1) * 32)
                beyond_first(pe, a_max, n)
                q, k = stack
                nc.tensor.matmul(bank[0].rearrange("p (g k) -> p g k", g=GRP), identb[:, :],
                                 mask_q[:, :].unsqueeze(1).to_broadcast([P, GRP, P]), start=True, stop=False)
                for a in range(2):
                    nc.tensor.matmul(bank[1 + a].rearrange("p (g k) -> p g k", g=2)[:, :, P:T], identb[:, :],
                                     mask_q[:, :].unsqueeze(1).to_broadcast([P, 2, P]), start=True, stop=False)
                for g in range(GRP):
                    r, pair, m, o = head(t, s, g)
                    nc.tensor.matmul(bank[0][:, g * P:(g + 1) * P], q[r, pair, m, o:o + P], k[r, pair, m, o:o + P],
                                     start=False, stop=g == GRP - 1)
                for g in range(GRP):
                    r, pair, m, o = head(t, s, g)
                    for kt in range(QT):
                        c = g % 2 * T + kt * P
                        last = nc.tensor.matmul(bank[1 + g // 2][:, c:c + P], q[r, pair, m, o + P:o + T], k[r, pair, m, o + kt * P:o + (kt + 1) * P],
                                                start=False, stop=g % 2 == 1 and kt == 1)
                last.then_inc(a_s, 1)

            def max_T(t, s):
                n = t * UNITS + s
                pe.wait_ge(a_max, n + 1)
                for qt in range(QT):
                    last = nc.tensor.matmul(bank[7][0:3 * GRP, qt * P:(qt + 1) * P], mparts[:, qt, :, :].rearrange("p a g -> p (a g)"),
                                            identb[:, :], start=True, stop=True)
                last.then_inc(a_mTp, 1)

            def weights(t, s):
                n = t * UNITS + s
                pe.wait_ge(a_mT, n + 1)
                beyond_first(pe, a_exp, n)
                q, k = stack
                for g in range(GRP):
                    nc.tensor.matmul(bank[3 + g // 2][:, g % 2 * T:(g % 2 + 1) * T], select[:, g, :], mT[:, s % 2, :], start=g % 2 == 0, stop=False)
                    nc.tensor.matmul(bank[5][:, g * P:(g + 1) * P], select[:, g, :], mT[:, s % 2, P:T], start=g == 0, stop=False)
                for a in range(2):
                    nc.tensor.matmul(bank[3 + a].rearrange("p (g k) -> p g k", g=2)[:, :, 0:P], identb[:, :],
                                     mask_k[:, :].unsqueeze(1).to_broadcast([P, 2, P]), start=False, stop=False)
                nc.tensor.matmul(bank[5].rearrange("p (g k) -> p g k", g=GRP), identb[:, :],
                                 mask_k[:, :].unsqueeze(1).to_broadcast([P, GRP, P]), start=False, stop=False)
                for g in range(GRP):
                    r, pair, m, o = head(t, s, g)
                    nc.tensor.matmul(bank[3 + g // 2][:, g % 2 * T:(g % 2 + 1) * T], k[r, pair, m, o:o + P], q[r, pair, m, o:o + T],
                                     start=False, stop=g % 2 == 1)
                for g in range(GRP):
                    r, pair, m, o = head(t, s, g)
                    last = nc.tensor.matmul(bank[5][:, g * P:(g + 1) * P], k[r, pair, m, o + P:o + T], q[r, pair, m, o + P:o + T],
                                            start=False, stop=g == GRP - 1)
                last.then_inc(a_st, 1)

            def weigh_values(t, s):
                n, v, j = t * UNITS + s, s // GRP, s % GRP
                pe.wait_ge(a_exp, n + 1)
                if j == 0:
                    pe.wait_ge(a_ysum, t * SLOTS + (v + 1))
                    if v % 2 == 0:
                        pe.wait_ge(a_vs, t * 2 + (v // 2 + 1))
                for g in range(GRP):
                    r, c = g % 2 * HALF, g // 2 * T
                    for kt in range(QT):
                        of_head = vz[:, (v * QT + kt) * GRP + g, j * HALF:(j + 1) * HALF]
                        w = pT[:, s % 2, g * T:(g + 1) * T] if kt == 0 else pT[:, s % 2, GRP * T + g * P:GRP * T + (g + 1) * P]
                        last = nc.tensor.matmul(bank[6][r:r + HALF, c + kt * P:c + T], of_head, w,
                                                start=j == 0 and g < 2 and kt == 0, stop=j == GRP - 1 and g >= 2 and kt == 1)
                last.then_inc(a_pv, 1)

            def project_out(b):
                pe.wait_ge(a_y, b * 2 + 4)
                for i in range(QT):
                    o = bank[7][:, i * C:(i + 1) * C]
                    nc.tensor.matmul(o, ones[0:3, :], bias3[:, E * EW + C:E * EW + 2 * C], start=True, stop=False)
                    last = nc.tensor.matmul(o, yT[:, i * P:(i + 1) * P], w_out[:, :], start=False, stop=True)
                last.then_inc(a_proj, 1)

            rows_T(0)
            project(0, 0)
            pe.wait_ge(a_rest[0], 1)
            project(1, 0)
            pe.wait_ge(a_rest[1], 1)
            values(0)
            pe.wait_ge(a_vs, 1)
            rows_T(1)
            scores(0, 0)
            scores(0, 1)
            pe.wait_ge(a_xT, 2)
            max_T(0, 0)

            def bank7_read(t, s):
                steps = Steps(t, s)
                for step, sem_read in ((steps.q, a_rest[0]), (steps.k, a_rest[1]), (steps.v, a_vs), (steps.x, a_xT)):
                    if step is not None:
                        pe.wait_ge(sem_read, step + 1)
                if steps.project is not None:
                    pe.wait_ge(a_x2, steps.project + 2)

            def last_turn(t):
                return isinstance(t, int) and t == TURNS_A - 1

            def bank7_free(t, s):
                if last_turn(t) and router_step(s, 2) is not None:
                    pe.wait_ge(s_xnT, NQ + router_step(s, 2) + 1)
                elif last_turn(t) and (router_step(s, 3) is not None or router_step(s, 5) is not None):
                    pe.wait_ge(s_read, read_until(s))
                else:
                    bank7_read(t, s)

            def unit(t, s):
                t0, s0 = t, s
                t, s = t + s // UNITS, s % UNITS
                n = t * UNITS + s
                steps = Steps(t, s)
                if steps.scores_next:
                    scores(*after(t, s, 2))
                if steps.max_next:
                    if s0 > 0:
                        bank7_free(*after(t0, s0 - 1, 0))
                    else:
                        pe.wait_ge(a_mT, 1)
                    max_T(*after(t, s, 1))
                weights(t, s)
                if steps.max_next:
                    pe.wait_ge(a_mT, n + 2)
                elif s0 > 0:
                    bank7_free(*after(t0, s0 - 1, 0))
                if steps.q is not None:
                    project(0, steps.q)
                if steps.k is not None:
                    project(1, steps.k)
                if steps.v is not None:
                    values(steps.v)
                if steps.x is not None:
                    rows_T(steps.x)
                if steps.project is not None:
                    project_out(steps.project)
                if s0 > 0:
                    weigh_values(*after(t0, s0 - 1, 0))
                if last_turn(t) and any(router_step(s, first) is not None for first in (2, 3, 5)):
                    bank7_read(t, s)
                    router(s)

            attention_loop(pe, unit, None)
            weigh_values(TURNS_A - 1, UNITS - 1)
            bank7_free(TURNS_A - 1, UNITS - 1)
            project_out(B - 1)

        @block.tensor
        def _(pe):
            pe.wait_ge(s_const, 48)
            for f in range(2):
                def transposes(q):
                    pe.wait_ge(s_xn, f * NQ + q + 1)
                    if q >= 2:
                        pe.wait_ge(s_xnT, f * NQ + q - 1)
                    to = bank[7] if merged(f, q) else bank[q % 2]
                    for i in range(QUAD):
                        last = nc.tensor.transpose(to[:, i * P:(i + 1) * P], rows_of(f, q)[:, i, 0, 0:C], ident)
                    last.then_inc(s_xnTp, 1)

                def logits(q):
                    pe.wait_ge(s_xnT, f * NQ + q + 1)
                    if q >= 2:
                        pe.wait_ge(s_mask, f * NQ + q - 1)
                    for i in range(QUAD):
                        last = nc.tensor.matmul(logits_bank(f, q)[:, i * E:(i + 1) * E], xnT_of(f, q)[:, i * P:(i + 1) * P], wg[:, :],
                                                start=True, stop=True)
                    last.then_inc(s_logit, 1)

                def ranks(q):
                    if q == 0 and f == 0:
                        pe.wait_ge(s_setup, 1)
                    pe.wait_ge(s_mask, f * NQ + q + 1)
                    if q >= 2:
                        pe.wait_ge(s_pos, f * NQ + q - 1)
                    o = ranks_bank(f, q)
                    nc.tensor.matmul(o, tri[:, :], mask[:, QUAD * q:QUAD * q + QUAD, :].rearrange("p n e -> p (n e)"), start=True, stop=False)
                    for i in range(QUAD - 1):
                        n = QUAD - 1 - i
                        nc.tensor.matmul(o[:, (i + 1) * E:].rearrange("p (n e) -> p n e", n=n), ones[:, :],
                                         mask[:, QUAD * q + i, :].unsqueeze(1).to_broadcast([P, n, E]), start=False, stop=False)
                    nc.tensor.matmul(o.rearrange("p (n e) -> p n e", n=QUAD), ones[:, :],
                                     macc[:, q, :].unsqueeze(1).to_broadcast([P, QUAD, E]), start=False, stop=True).then_inc(s_rank, 1)

                def router(s):
                    if router_step(s, 2) is not None:
                        transposes(router_step(s, 2))
                    if router_step(s, 3) is not None:
                        logits(router_step(s, 3))
                    if router_step(s, 5) is not None:
                        ranks(router_step(s, 5))

                if f == 1:
                    attention_tensor(pe, router)
                for q in range(f * MERGED, NQ + 1):
                    if q < NQ:
                        transposes(q)
                        logits(q)
                    if q > f * MERGED:
                        ranks(q - 1)
                nc.tensor.matmul(bank[6][0:E, 0:P], macc[:, NQ, :], ones[:, :], start=True, stop=True).then_inc(s_count, 1)
                pe.wait_ge(s_ntile, f + 1)
                nc.tensor.matmul(bank[7][:, 0:2 * E], ntile[:, :], utri[:, :], start=True, stop=True).then_inc(s_cum, 1)

                pe.wait_ge(s_tab, 32 * (f + 1))
                if f == 0:
                    pe.wait_ge(s_wexp, 32)
                    pe.wait_ge(s_bias3, 80 + 48)

                held = {}

                def offsets(t, k):
                    key = (t if isinstance(t, int) else str(t), k // 2)
                    if key not in held:
                        held[key] = registers(nc, pe, tab[0:1, bass.ds(t * UNROLL + k // 2 * 4, 4)], (E - 1) * EW)
                    return held[key][k % 2 * 2:k % 2 * 2 + 2]

                def turn_x(t, k):
                    n = t * DUOS + k + f * PAIRS
                    for i in range(2):
                        pe.wait_ge(s_xt[2 * k + i], (t + 1 + f * TURNS) * 16)
                    for i in range(2):
                        last = nc.tensor.transpose(bank[k % 2][:, i * P:(i + 1) * P], xt[:, 2 * k + i, 0:C], ident)
                    last.then_inc(s_xTp, 1)

                def gate_up(t, k):
                    n = t * DUOS + k + f * PAIRS
                    e = offsets(t, k)
                    pe.wait_ge(s_xT, n + 1)
                    for i in range(2):
                        o = bank[2 + k % 2][:, i * 2 * F:(i + 1) * 2 * F]
                        nc.tensor.matmul(o, ones[0:3, :], bias3[:, bass.ds(e[i], 2 * F)], start=True, stop=False)
                        last = nc.tensor.matmul(o, xT[:, k % 2, i * P:(i + 1) * P], w_all[:, bass.ds(e[i], 2 * F)],
                                                start=False, stop=True)
                    last.then_inc(s_gu, 1)

                def turn_g(t, k):
                    n = t * DUOS + k + f * PAIRS
                    pe.wait_ge(s_gated, n + 1)
                    for i in range(2):
                        last = nc.tensor.transpose(bank[4 + k % 2][:, i * P:(i + 1) * P], upc[:, k % 2, i, :], ident)
                    last.then_inc(s_gTp, 1)

                def down(t, k):
                    n = t * DUOS + k + f * PAIRS
                    e = offsets(t, k)
                    pe.wait_ge(s_gT, n + 1)
                    beyond_first(pe, s_ysb[(k + 2) % DUOS], t + (k // 2 + f * TURNS))
                    for i in range(2):
                        o = bank[6 + k % 2][:, i * C:(i + 1) * C]
                        nc.tensor.matmul(o, ones[0:3, :], bias3[:, bass.ds(e[i] + 2 * F, C)], start=True, stop=False)
                        last = nc.tensor.matmul(o, gT[:, k % 2, i * P:(i + 1) * P], w_all[:, bass.ds(e[i] + 2 * F, C)],
                                                start=False, stop=True)
                    last.then_inc(s_y, 1)

                expert_pipeline(pe, turn_x, gate_up, turn_g, down)


class Steps:

    def __init__(self, t, s):
        v, j = s // GRP, s % GRP
        b = t * SLOTS + v
        last = isinstance(t, int) and t == TURNS_A - 1
        half = v // 2
        self.half = 1 - half

        def pair(ahead):
            x = t * 2 + half + ahead
            return x if not isinstance(x, int) or x < B // 2 else None

        self.scores_next = not last or s + 2 < UNITS
        self.max_next = not last or s + 1 < UNITS
        self.q = self.k = self.v = self.x = self.sums = self.project = None
        self.divide = self.add = self.combine = self.normalise = None
        if v % 2 == 0:
            if j == 0:
                self.q = pair(1)
            if j == 1:
                self.k = pair(1)
            if j == 3:
                self.combine = pair(2)
        else:
            if j == 0:
                self.v, self.normalise = pair(1), pair(2)
            if j == 1:
                self.x = pair(2)
        if j == 0 and (not isinstance(b, int) or b > 0):
            self.sums = b - 1
        if j in (1, 2):
            self.divide = b - 1
        if j == 3:
            self.project = self.add = b - 1


def after(t, s, ahead):
    return t + (s + ahead) // UNITS, (s + ahead) % UNITS


def attention_loop(eng, unit, chain):
    unit(0, 0)
    with eng.Fori(0, TURNS_A - 1) as t:
        if chain:
            chain[0].begin(t, chain[1])
        for s in range(1, UNITS + 1):
            unit(t, s)
    if chain:
        chain[0].end(TURNS_A - 1)
    for s in range(1, UNITS):
        unit(TURNS_A - 1, s)


ATT_CHAIN = 116


def registers(nc, eng, table, most):
    return nc.values_load_multi_w_load_instructions(table, engines=[eng.engine], min_val=0, max_val=most,
                                                    skip_runtime_bounds_check_because="the table is made on the chip")[1]


def beyond_first(eng, sem, value):
    if not isinstance(value, int) or value > 0:
        eng.wait_ge(sem, value)


def expert_pipeline(eng, first, second, third, fourth):
    steps = ((0, first), (1, second), (3, fourth), (2, third))

    def slot(t, k, from_turn, to_turn):
        for behind, step in steps:
            pair = k - behind
            turn, k2 = t + pair // DUOS, pair % DUOS
            if isinstance(turn, int) and not from_turn <= turn < to_turn:
                continue
            step(turn, k2)

    def turn(t):
        for k in range(DUOS):
            slot(t, k, 0, TURNS)

    turn(0)
    turn(1)
    with eng.Fori(2, TURNS) as t:
        turn(t)
    for k in range(len(steps) - 1):
        slot(TURNS, k, 0, TURNS)


_OUT = (B, T, C)


def kernel(**inputs):
    import concourse.bacc as bacc
    from concourse.bass_utils import run_bass_kernel_spmd

    w = {k: np.asarray(v) for k, v in inputs.items()}
    parts = {
        "x": w["L0_attn_x"].reshape(N, C),
        "w_g": w["L0_ffn_Wg"].T,
        "b_g": w["L0_ffn_bg"],
        "w_gu": w["L0_ffn_Wgu"].reshape(E, C, F, 2).transpose(1, 0, 3, 2).reshape(C, E * 2 * F),
        "w_d": w["L0_ffn_Wd"].transpose(1, 0, 2).reshape(F, E * C),
        "b_gu": w["L0_ffn_bgu"].reshape(E, F, 2).transpose(0, 2, 1).reshape(E, 2 * F),
        "b_d": w["L0_ffn_bd"],
        "b_attn": w["L0_attn_b_attn"].reshape(3, C),
        "b_proj": w["L0_attn_b_proj"].reshape(1, C),
        "w_attn": w["L0_attn_W_attn"],
        "w_proj": w["L0_attn_W_proj"],
        "konst": shape_constants(),
    }
    nc = bacc.Bacc("TRN2", target_bir_lowering=False, num_devices=1)
    arrays, aps = {}, {}
    for name, a in parts.items():
        arrays[f"in_{name}"] = np.ascontiguousarray(a)
        aps[name] = nc.dram_tensor(f"in_{name}", a.shape, mybir.dt.from_np(a.dtype), kind="ExternalInput").ap()
    out = nc.dram_tensor("out", (N, C), F32, kind="ExternalOutput").ap()
    build_block(nc, out=out, **aps)
    r = run_bass_kernel_spmd(nc, [arrays], core_ids=[0])
    return r.results[0]["out"].reshape(_OUT)
```
